# Optimizing a Trainium2 kernel written in Bass

```python
import numpy as np
import jax
import jax.numpy as jnp

def _softmax(x, axis=-1):
    return jax.nn.softmax(x, axis=axis)

def _gelu(x):
    return jax.nn.gelu(x, approximate=True)

def _silu(x):
    return jax.nn.silu(x)

def _sigmoid(x):
    return jax.nn.sigmoid(x)

def _layernorm(x, axis=-1, eps=1e-05):
    m = jnp.mean(x, axis=axis, keepdims=True)
    v = jnp.var(x, axis=axis, keepdims=True)
    return (x - m) / jnp.sqrt(v + eps)

def _scatter_add(tgt, idx, src, axis=0):
    return tgt.at[idx].add(src)

def _segment_sum(src, seg, n):
    return jax.ops.segment_sum(src, seg, n)
kernel_name = 'mk_prb_d1_jaxref_r4_249968'

def setup_inputs(seed: int=0):
    np.random.seed(seed)
    _w = jnp.asarray

    def _L0_attn_setup():
        import math
        import jax, jax.numpy as jnp
        import numpy as np
        B, T, D = (8, 512, 256)

        def _gelu(x):
            c = math.sqrt(2.0 / math.pi)
            return 0.5 * x * (1.0 + jnp.tanh(c * (x + 0.044715 * x * x * x)))

        def _normalize(x, axis):
            n = jnp.linalg.norm(x, axis=axis, keepdims=True)
            return x / jnp.maximum(n, 1e-12)
        key = jax.random.key(seed)
        k1, k2 = jax.random.split(key)
        x = jax.random.normal(k1, (B, T, D), dtype=jnp.float32)
        ema_out = _normalize(jax.random.normal(k2, (D,), dtype=jnp.float32), 0)[..., 0] if False else None
        ema = jax.random.normal(k2, (D,), dtype=jnp.float32)
        ema = ema / jnp.maximum(jnp.linalg.norm(ema), 1e-12)
        return {'x': x, 'ema_out': ema, 'logit_decay': jnp.float32(math.log(0.9 / 0.1)), 'log_tau': jnp.float32(math.log(2.0)), 'log_blend': jnp.float32(math.log(0.3 / 0.7)), 'logit_blend_seq': jnp.float32(0.0)}
    _L0_attn_in = _L0_attn_setup()

    def _L0_ffn_setup():
        import jax, jax.numpy as jnp
        import numpy as np
        B, S, D = (4, 512, 256)
        P = 9
        DM = D // 4
        EPS = 1e-05

        def _mix(x, mix_kernel):
            xp = jnp.pad(x, ((0, 0), (1, 1), (0, 0)))
            return mix_kernel[0] * xp[:, :-2] + mix_kernel[1] * xp[:, 1:-1] + mix_kernel[2] * xp[:, 2:]

        def _layernorm(h, gamma, beta):
            mu = jnp.mean(h, axis=-1, keepdims=True)
            var = jnp.var(h, axis=-1, keepdims=True)
            return (h - mu) * jax.lax.rsqrt(var + EPS) * gamma + beta
        key = jax.random.key(seed)
        ks = jax.random.split(key, 12)
        sc_in = 1.0 / np.sqrt(D)
        sc_mid = 1.0 / np.sqrt(DM)
        return {'x': jax.random.normal(ks[0], (B, S, D), dtype=jnp.float32), 'mix_kernel': jax.random.normal(ks[1], (3, D), dtype=jnp.float32) * 0.5, 'W1': jax.random.normal(ks[2], (P, D, DM), dtype=jnp.float32) * sc_in, 'b1': jnp.zeros((P, DM), dtype=jnp.float32), 'W2': jax.random.normal(ks[3], (P, DM, D), dtype=jnp.float32) * sc_mid, 'b2': jnp.zeros((P, D), dtype=jnp.float32), 'Wo1': jax.random.normal(ks[4], (D, DM), dtype=jnp.float32) * sc_in, 'bo1': jnp.zeros((DM,), dtype=jnp.float32), 'Wo2': jax.random.normal(ks[5], (DM, P), dtype=jnp.float32) * sc_mid, 'bo2': jnp.zeros((P,), dtype=jnp.float32), 'gamma': jnp.ones((D,), dtype=jnp.float32), 'beta': jnp.zeros((D,), dtype=jnp.float32)}
    _L0_ffn_in = _L0_ffn_setup()
    _d = {'L0_attn_x': _L0_attn_in['x'], 'L0_attn_ema_out': _L0_attn_in['ema_out'], 'L0_attn_logit_decay': _L0_attn_in['logit_decay'], 'L0_attn_log_tau': _L0_attn_in['log_tau'], 'L0_attn_log_blend': _L0_attn_in['log_blend'], 'L0_attn_logit_blend_seq': _L0_attn_in['logit_blend_seq'], 'L0_ffn_mix_kernel': _L0_ffn_in['mix_kernel'], 'L0_ffn_W1': _L0_ffn_in['W1'], 'L0_ffn_b1': _L0_ffn_in['b1'], 'L0_ffn_W2': _L0_ffn_in['W2'], 'L0_ffn_b2': _L0_ffn_in['b2'], 'L0_ffn_Wo1': _L0_ffn_in['Wo1'], 'L0_ffn_bo1': _L0_ffn_in['bo1'], 'L0_ffn_Wo2': _L0_ffn_in['Wo2'], 'L0_ffn_bo2': _L0_ffn_in['bo2'], 'L0_ffn_gamma': _L0_ffn_in['gamma'], 'L0_ffn_beta': _L0_ffn_in['beta']}
    _x0 = _d['L0_attn_x']
    _d['L0_attn_x'] = jax.random.normal(jax.random.fold_in(jax.random.key(seed), 1), (4, 1024, 256), dtype=_x0.dtype)
    del _x0
    return _d

def reference(L0_attn_x, L0_attn_ema_out, L0_attn_logit_decay, L0_attn_log_tau, L0_attn_log_blend, L0_attn_logit_blend_seq, L0_ffn_mix_kernel, L0_ffn_W1, L0_ffn_b1, L0_ffn_W2, L0_ffn_b2, L0_ffn_Wo1, L0_ffn_bo1, L0_ffn_Wo2, L0_ffn_bo2, L0_ffn_gamma, L0_ffn_beta):

    def _L0_attn_ref(x, ema_out, logit_decay, log_tau, log_blend, logit_blend_seq):
        import math
        import jax, jax.numpy as jnp
        import numpy as np
        B, T, D = (8, 512, 256)

        def _gelu(x):
            c = math.sqrt(2.0 / math.pi)
            return 0.5 * x * (1.0 + jnp.tanh(c * (x + 0.044715 * x * x * x)))

        def _normalize(x, axis):
            n = jnp.linalg.norm(x, axis=axis, keepdims=True)
            return x / jnp.maximum(n, 1e-12)
        Bx, Tx, Dx = x.shape
        tau = jnp.exp(log_tau)
        alpha = jax.nn.sigmoid(log_blend)
        w_seq = jax.nn.sigmoid(logit_blend_seq)
        out = _gelu(x)
        out_norm = _normalize(out, -1)
        ema_norm = ema_out / jnp.maximum(jnp.linalg.norm(ema_out), 1e-12)
        ema_sim = jnp.einsum('btd,d->bt', out_norm, ema_norm)
        sim_mat = jnp.einsum('btd,bsd->bts', out_norm, out_norm)
        causal = jnp.tril(jnp.ones((Tx, Tx), dtype=bool), k=-1)
        sim_past = jnp.where(causal[None], sim_mat, -2.0)
        seq_sim = jnp.max(sim_past, axis=-1)
        has_past = (jnp.arange(Tx) > 0)[None, :]
        seq_sim = jnp.where(has_past, seq_sim, ema_sim)
        familiarity = w_seq * seq_sim + (1.0 - w_seq) * ema_sim
        novelty = jnp.exp(-tau * familiarity)
        gate = 1.0 - alpha + alpha * novelty
        return out * gate[..., None]

    def _L0_ffn_ref(x, mix_kernel, W1, b1, W2, b2, Wo1, bo1, Wo2, bo2, gamma, beta):
        import jax, jax.numpy as jnp
        import numpy as np
        B, S, D = (4, 512, 256)
        P = 9
        DM = D // 4
        EPS = 1e-05

        def _mix(x, mix_kernel):
            xp = jnp.pad(x, ((0, 0), (1, 1), (0, 0)))
            return mix_kernel[0] * xp[:, :-2] + mix_kernel[1] * xp[:, 1:-1] + mix_kernel[2] * xp[:, 2:]

        def _layernorm(h, gamma, beta):
            mu = jnp.mean(h, axis=-1, keepdims=True)
            var = jnp.var(h, axis=-1, keepdims=True)
            return (h - mu) * jax.lax.rsqrt(var + EPS) * gamma + beta
        x_mixed = _mix(x, mix_kernel)
        h = jnp.einsum('bsd,pdm->bspm', x_mixed, W1) + b1
        stacked_paths = jnp.einsum('bspm,pmd->bspd', h, W2) + b2
        scores = jnp.tanh(x_mixed @ Wo1 + bo1) @ Wo2 + bo2
        idx = jnp.argmax(scores, axis=-1)
        weights = jax.nn.one_hot(idx, P, dtype=stacked_paths.dtype)
        collapsed = jnp.einsum('bspd,bsp->bsd', stacked_paths, weights)
        return _layernorm(x + collapsed, gamma, beta)
    x = L0_attn_x
    xn = _layernorm(x, axis=-1)
    x = x + _L0_attn_ref(xn, L0_attn_ema_out, L0_attn_logit_decay, L0_attn_log_tau, L0_attn_log_blend, L0_attn_logit_blend_seq) + _L0_ffn_ref(xn, L0_ffn_mix_kernel, L0_ffn_W1, L0_ffn_b1, L0_ffn_W2, L0_ffn_b2, L0_ffn_Wo1, L0_ffn_bo1, L0_ffn_Wo2, L0_ffn_bo2, L0_ffn_gamma, L0_ffn_beta)
    return x

_drawn_inputs = setup_inputs


def setup_inputs(seed=0):
    import zlib

    import numpy as np

    out = dict(_drawn_inputs(seed))
    spreads = {'L0_ffn_b1': (0.0, 0.1),
     'L0_ffn_b2': (0.0, 0.1),
     'L0_ffn_bo1': (0.0, 0.1),
     'L0_ffn_bo2': (0.0, 0.1),
     'L0_ffn_gamma': (1.0, 0.2),
     'L0_ffn_beta': (0.0, 0.1)}
    factors = {}
    for name, (base, spread) in spreads.items():
        noise = np.random.default_rng([zlib.crc32(name.encode()), seed]).standard_normal(out[name].shape)
        drawn = base * np.exp(spread * noise) if base else spread * noise
        out[name] = jnp.asarray(drawn.astype(out[name].dtype))
    for name, factor in factors.items():
        out[name] = (out[name] * factor).astype(out[name].dtype)
    return out
```

```python
from contextlib import ExitStack

import concourse.bass as bass
from concourse import mybir

F32 = mybir.dt.float32
F16 = mybir.dt.float16
ALU = mybir.AluOpType
ACT = mybir.ActivationFunctionType
AX = mybir.AxisListType
RMAX = bass.bass_isa.ReduceOp.max

P = 128
LN_EPS = 1e-5
NORM_MIN = 1e-12
SCALE_MIN = 1e-4
NATURAL = 2.718281828459045


def build(nc, x, ema, log_tau, log_blend, logit_seq, mix_k, W1, b1, W2, b2, Wo1, bo1, Wo2, bo2,
          gamma, beta, out):
    B, T, D = x.shape
    E, _, M = W1.shape
    NT = T // P
    KD = D // P
    GT = 4
    NG = NT // GT
    GW = GT * P
    NJ = E // 2
    NH = NJ + 1
    EM = E * M
    PAD = 32
    CHUNKS = NG * KD
    PIECES = [(t, 0, min(t + 1, 4)) for t in range(4)]
    PIECES += [p for t in range(4, NT) for p in ((t, 0, 4), (t, 4, t + 1))]
    NP = len(PIECES)

    ctx = ExitStack()
    with ctx:
        def sb(name, shape, dt=F32):
            return ctx.enter_context(nc.sbuf_tensor(name, shape, dt))

        def ps(name, shape, dt=F32):
            return ctx.enter_context(nc.psum_tensor(name, shape, dt))

        def sem(name):
            return ctx.enter_context(nc.semaphore(name))

        ident = sb("ident", [P, P])
        ident16 = sb("ident16", [P, P], F16)
        future16 = sb("future16", [P, P], F16)
        prio = sb("prio", [P, GT, E])
        mhalf = sb("mhalf", [P, NT])
        e_base = sb("e_base", [P, NT])
        first_row = sb("first_row", [P, 1])
        not_first = sb("not_first", [P, 1])
        knobs = sb("knobs", [P, 3])
        tau = sb("tau", [P, 8])
        kmix = sb("kmix", [P, 3, KD])
        kabs = sb("kabs", [P, KD])
        ema_n = sb("ema_n", [P, 2])
        ema_col = sb("ema_col", [P, KD])
        ema_hl = sb("ema_hl", [P, KD, 2], F16)
        mixt = sb("mixt", [P, CHUNKS, GW])
        spare = mixt[:, :, :].rearrange("p c w -> p (c w)").rearrange("p (j d) -> p j d", d=D)
        w2s = spare[:, 0:NJ + 1, :]
        b2s = spare[:, NJ + 1, :]
        ema_row = spare[:, NJ + 2, :]
        ema_sq = spare[:, NJ + 3, :]
        z = sb("z", [P, NG, GT, D])
        w1s = z[:, :, :, :].rearrange("p g t d -> p (g t d)")[:, 0:KD * (EM + M)].rearrange("p (k c) -> p k c", k=KD)
        w1h = sb("w1h", [P, KD, EM + M], F16)
        w1l = sb("w1l", [P, KD, EM + M], F16)
        w2h = sb("w2h", [P, NJ + 1, D], F16)
        w2l = sb("w2l", [P, NJ, D], F16)
        b2h = sb("b2h", [P, D], F16)
        tailB = sb("tailB", [P, D], F16)
        b1s = sb("b1s", [P, NJ + 1])
        bo1s = sb("bo1s", [P, 1])
        wo2s = sb("wo2s", [P, E])
        bo2r = sb("bo2r", [P, E])
        gam = sb("gam", [P, D])
        bet = sb("bet", [P, D])
        amax = sb("amax", [P, 6])
        gmax = sb("gmax", [P, 6])
        sc = sb("sc", [P, 24])

        x_sb = sb("x_sb", [P, B, NT, D])
        out_sb = sb("out_sb", [P, B, NT, D])
        uT = sb("uT", [P, B, 2 * KD, T], F16)
        xmT = sb("xmT", [P, B, 2 * KD, T], F16)
        mv = sb("mv", [P, NT, 2])
        var_e = sb("var_e", [P, NT])
        rstd_s = sb("rstd_s", [P, NT])
        rstd = sb("rstd", [P, B, NT])
        nbias = sb("nbias", [P, NT])
        ss = sb("ss", [P, NT])
        ss_b = sb("ss_b", [P, NT])
        rnorm = sb("rnorm", [P, NT])
        expo = sb("expo", [P, NT])
        gate = sb("gate", [P, NT])

        stats = sb("stats", [P, NT, 6])
        xn_st = sb("xn_st", [P, 4, D])
        junk = sb("junk", [P, 2, D], F16)
        uh_st = sb("uh_st", [P, 2, D], F16)
        ul_st = sb("ul_st", [P, 2, D], F16)
        xnT = sb("xnT", [P, KD, T + 2])

        smax = sb("smax", [P, NT, 2])
        seq = sb("seq", [P, NT])
        ems = sb("ems", [P, NT])
        fix = sb("fix", [P, 1])
        novelty = sb("novelty", [P, NT])

        sT = sb("sT", [P, GW])
        sco = sb("sco", [P, GT, E])
        top = sb("top", [P, GT, 2])
        ohp = sb("ohp", [P, GT, PAD], F16)
        ohT = sb("ohT", [PAD, GW], F16)
        pick = sb("pick", [PAD, NH, P], F16)
        mask_sb = sb("mask_sb", [P, 2, GW], F16)
        hm = sb("hm", [P, 2, GW])
        hh = sb("hh", [P, NG, NJ, GW], F16)
        hl = sb("hl", [P, NG, NJ, GW], F16)
        tA = sb("tA", [P, NG, GW], F16)
        tB = sb("tB", [P, NG, GW], F16)
        rc = sb("rc", [P, NG, GT])
        zst = sb("zst", [P, GT, 6])
        zmv = sb("zmv", [P, NG, GT, 2])
        zve = sb("zve", [P, NG, GT])
        zr = sb("zr", [P, NG, GT])
        zb = sb("zb", [P, NG, GT])

        simP = [ps(f"simP{i}", [P, 512]) for i in range(2)]
        trP = ps("trP", [P, 512])
        trU = trP[:, 0:256].bitcast(F16).rearrange("p (c q) -> p c q", c=2 * KD)
        trX = trP[:, 256:512].rearrange("p (k q) -> p k q", k=KD)
        hP = [ps(f"hP{i}", [P, GW]) for i in range(2)]
        maskP = ps("maskP", [P, GW])
        yP = ps("yP", [P, D])
        miscP = ps("miscP", [P, 512])
        scoP = miscP[:, 0:GT * E].rearrange("p (i e) -> p i e", i=GT)
        emaP = miscP[:, 64:64 + 2 * NT].rearrange("p (t c) -> p t c", c=2)

        settled = sem("settled")
        w_loaded = sem("w_loaded")
        x_loaded = sem("x_loaded")
        pool_c = sem("pool_c")
        consts = sem("consts")
        amax_ready = sem("amax_ready")
        gmax_ready = sem("gmax_ready")
        knobs_in = sem("knobs_in")
        knobs_exp = sem("knobs_exp")
        ema_ss = sem("ema_ss")
        ema_rn = sem("ema_rn")
        dve_setup = sem("dve_setup")
        weights_ready = sem("weights_ready")

        st_ready = sem("st_ready")
        mv_ready = sem("mv_ready")
        var_ready = sem("var_ready")
        rstd_kept = sem("rstd_kept")
        rstd_ready = sem("rstd_ready")
        nb_ready = sem("nb_ready")
        xn_ready = sem("xn_ready")
        gelu_done = sem("gelu_done")
        tx_done = sem("tx_done")
        xe_done = sem("xe_done")
        ss_ready = sem("ss_ready")
        ss_bounded = sem("ss_bounded")
        rn_ready = sem("rn_ready")
        uh_ready = sem("uh_ready")
        ul_ready = sem("ul_ready")
        tu_done = sem("tu_done")
        ue_done = sem("ue_done")
        m0_done = sem("m0_done")
        m1_done = sem("m1_done")
        m2_done = sem("m2_done")
        xh_done = sem("xh_done")
        xl_done = sem("xl_done")

        sim_ready = sem("sim_ready")
        sim_free = sem("sim_free")
        ema_ready = sem("ema_ready")
        fam_c = sem("fam_c")
        expo_ready = sem("expo_ready")
        nov_ready = sem("nov_ready")
        gate_ready = sem("gate_ready")

        h_ready = sem("h_ready")
        tanh_done = sem("tanh_done")
        sco_ready = sem("sco_ready")
        arg_c = sem("arg_c")
        oh_ready = sem("oh_ready")
        ohTP_ready = sem("ohTP_ready")
        ohT_ready = sem("ohT_ready")
        maskP_ready = sem("maskP_ready")
        mask_ready = sem("mask_ready")
        hm_done = sem("hm_done")
        hi_done = sem("hi_done")
        lo_done = sem("lo_done")
        y_ready = sem("y_ready")
        z_done = sem("z_done")
        zs_c = sem("zs_c")
        zmv_ready = sem("zmv_ready")
        zve_ready = sem("zve_ready")
        zr_ready = sem("zr_ready")
        w_norm = sem("w_norm")
        zb_ready = sem("zb_ready")
        pool_g = sem("pool_g")
        w_affine = sem("w_affine")
        a_done = sem("a_done")
        o_ready = sem("o_ready")
        stored = sem("stored")

        def need(eng, s, v):
            if not isinstance(v, int) or v > 0:
                eng.wait_ge(s, v)

        loads = [
            (knobs[:, 0:1], log_tau.partition_broadcast(P)),
            (knobs[:, 1:2], log_blend.partition_broadcast(P)),
            (knobs[:, 2:3], logit_seq.partition_broadcast(P)),
            (ema_row[:, :], ema.partition_broadcast(P)),
            (bo2r[:, :], bo2.partition_broadcast(P)),
            (gam[:, :], gamma.partition_broadcast(P)),
            (bet[:, :], beta.partition_broadcast(P)),
            (wo2s[M:2 * M, :], Wo2),
            (bo1s[M:2 * M, :], bo1.rearrange("(m o) -> m o", o=1)),
            (b1s[:, 0:NJ], b1[0:2 * NJ, :].rearrange("(j a) m -> (a m) j", a=2)),
            (b1s[0:M, NJ:NJ + 1], b1[E - 1:E, :].rearrange("o m -> m o")),
            (w2s[:, 0:NJ, :], W2[0:2 * NJ].rearrange("(j a) m d -> (a m) j d", a=2)),
            (w2s[0:M, NJ, :], W2[E - 1]),
            (w2s[M:2 * M, NJ, :], W2[E - 1]),
            (b2s[M:M + E, :], b2),
            (b2s[M + PAD:M + PAD + E, :], b2),
            (ema_col[:, :], ema.rearrange("(k p) -> p k", p=P)),
        ]
        for k in range(KD):
            loads += [
                (w1s[:, k, 0:EM].rearrange("p (e m) -> p e m", e=E),
                 W1[:, k * P:(k + 1) * P, :].rearrange("e p m -> p e m")),
                (w1s[:, k, EM:EM + M], Wo1[k * P:(k + 1) * P, :]),
                (kmix[:, :, k], mix_k[:, k * P:(k + 1) * P].rearrange("j p -> p j")),
            ]

        def settle(eng):
            eng.sem_inc(settled, 1)

        block = ctx.enter_context(nc.Block())

        def schedule(eng, front_stats, sim, front_tile, front_norm, gates, ffn, front_unit, front_mix):
            def front(n):
                front_stats(n)
                for t in range(NT):
                    front_tile(n, t)
                front_norm(n)
                front_unit(n)
                front_mix(n)

            def batch(b, following):
                if following is not None:
                    front_stats(following)
                for t in range(NT):
                    sim(b, t)
                    if following is not None:
                        front_tile(following, t)
                if following is not None:
                    front_norm(following)
                gates(b)
                ffn(b, 0)
                if following is not None:
                    front_unit(following)
                ffn(b, 1)
                if following is not None:
                    front_mix(following)

            front(0)
            with eng.Fori(0, B - 1) as b:
                batch(b, b + 1)
            batch(B - 1, None)

        def nothing(*_):
            pass

        @block.sync
        def _(sp):
            xv = x.rearrange("b (t p) d -> b p t d", p=P)
            sp.dma_start(x_sb[:, 0], xv[0]).then_inc(x_loaded, 16)
            sp.wait_ge(consts, 1)
            for dst, src in loads:
                sp.dma_start(dst, src, allow_slow_non_contiguous=True).then_inc(w_loaded, 16)
            for n in range(1, B):
                sp.wait_ge(x_loaded, 16 * n)
                sp.dma_start(x_sb[:, n], xv[n]).then_inc(x_loaded, 16)

            ov = out.rearrange("b (g t p) d -> b g p t d", p=P, t=GT)

            def ffn(b, g):
                sp.wait_ge(o_ready, NG * b + g + 1)
                sp.dma_start(ov[b, g], out_sb[:, b, g * GT:(g + 1) * GT]).then_inc(stored, 16)

            schedule(sp, nothing, nothing, nothing, nothing, nothing, ffn, nothing, nothing)
            sp.wait_ge(stored, 16 * NG * B)

        @block.gpsimd
        def _(pool):
            count = [0]

            def link(ins):
                count[0] += 1
                ins.then_inc(pool_c, 1)
                pool.wait_ge(pool_c, count[0])

            nc.gpsimd.memset(b1s[:, :], 0.0)
            nc.gpsimd.memset(amax[:, :], 0.0)
            nc.gpsimd.memset(b2s[:, :], 0.0).then_inc(consts, 1)
            nc.gpsimd.memset(xnT[:, :, 0:1], 0.0)
            nc.gpsimd.memset(xnT[:, :, T + 1:T + 2], 0.0)
            nc.gpsimd.memset(ohp[:, :, :], 0.0)
            nc.gpsimd.memset(smax[:, :, :], -8.0)
            nc.gpsimd.memset(mhalf[:, :], -0.5)
            nc.gpsimd.memset(e_base[:, :], NATURAL)
            nc.gpsimd.memset(first_row[:, :], 0.0)
            nc.gpsimd.memset(not_first[:, :], 1.0)
            nc.gpsimd.memset(future16[:, :], 0.0)
            nc.gpsimd.memset(ident16[:, :], 0.0)
            nc.gpsimd.memset(pick[:, :, :], 0.0)
            nc.gpsimd.iota(prio[:, :, :], pattern=[[0, GT], [-1, E]], base=E, channel_multiplier=0,
                           allow_small_or_imprecise_dtypes=True)
            link(nc.gpsimd.memset(ident[:, :], 0.0))
            nc.gpsimd.affine_select(out=ident[:, :], in_=ident[:, :], compare_op=ALU.not_equal, fill=1.0,
                                    base=0, pattern=[[-1, P]], channel_multiplier=1)
            nc.gpsimd.affine_select(out=ident16[:, :], in_=ident16[:, :], compare_op=ALU.not_equal, fill=1.0,
                                    base=0, pattern=[[-1, P]], channel_multiplier=1)
            nc.gpsimd.affine_select(out=pick[:, 0, 0:M], in_=pick[:, 0, 0:M], compare_op=ALU.not_equal, fill=1.0,
                                    base=1 - E, pattern=[[0, M]], channel_multiplier=1)
            own = pick[:, 0, M:P].rearrange("e (r c) -> e r c", c=PAD)
            nc.gpsimd.affine_select(out=own, in_=own, compare_op=ALU.not_equal, fill=1.0,
                                    base=0, pattern=[[0, 2], [-1, PAD]], channel_multiplier=1)
            pairs = pick[:, 1:NH, :].rearrange("e q (a m) -> e q a m", a=2)
            nc.gpsimd.affine_select(out=pairs, in_=pairs, compare_op=ALU.not_equal, fill=1.0,
                                    base=0, pattern=[[-2, NJ], [-1, 2], [0, M]], channel_multiplier=1)
            nc.gpsimd.affine_select(out=future16[:, :], in_=future16[:, :], compare_op=ALU.is_gt, fill=-4.0,
                                    base=0, pattern=[[-1, P]], channel_multiplier=1)
            nc.gpsimd.affine_select(out=first_row[:, :], in_=first_row[:, :], compare_op=ALU.not_equal, fill=1.0,
                                    base=0, pattern=[[0, 1]], channel_multiplier=1)
            nc.gpsimd.affine_select(out=not_first[:, :], in_=not_first[:, :], compare_op=ALU.not_equal, fill=0.0,
                                    base=0, pattern=[[0, 1]], channel_multiplier=1).then_inc(consts, 1)

            setup_done = [False]

            def setup():
                pool.wait_ge(amax_ready, 1)
                nc.gpsimd.partition_all_reduce(gmax[:, :], amax[:, :], P, RMAX).then_inc(gmax_ready, 1)
                pool.wait_ge(knobs_in, 1)
                nc.gpsimd.tensor_tensor(knobs[:, :], e_base[:, 0:3], knobs[:, :], ALU.pow).then_inc(knobs_exp, 1)
                pool.wait_ge(ema_ss, 1)
                nc.gpsimd.tensor_tensor(ema_n[:, 1:2], ema_n[:, 0:1], mhalf[:, 0:1], ALU.pow).then_inc(ema_rn, 1)

            def front_stats(n):
                pool.wait_ge(var_ready, n + 1)
                nc.gpsimd.tensor_tensor(rstd_s[:, :], var_e[:, :], mhalf[:, :], ALU.pow).then_inc(rstd_ready, 1)
                if not setup_done[0]:
                    setup_done[0] = True
                    setup()

            def front_norm(n):
                pool.wait_ge(ss_bounded, n + 1)
                nc.gpsimd.tensor_tensor(rnorm[:, :], ss_b[:, :], mhalf[:, :], ALU.pow).then_inc(rn_ready, 1)

            def gates(b):
                pool.wait_ge(expo_ready, b + 2)
                nc.gpsimd.tensor_tensor(novelty[:, :], e_base[:, :], expo[:, :], ALU.pow).then_inc(nov_ready, 1)

            def ffn(b, g):
                G = NG * b + g
                for q in range(NH):
                    H = NH * G + q
                    s = (NH * g + q) % 2
                    pool.wait_ge(hi_done, H + 1)
                    if q == 0:
                        nc.gpsimd.tensor_tensor(tA[M:2 * M, g], hm[0:M, s], tA[0:M, g],
                                                ALU.subtract).then_inc(lo_done, 1)
                    else:
                        if q == 1:
                            pool.wait_ge(lo_done, H + 2)
                        nc.gpsimd.tensor_tensor(hl[:, g, q - 1], hm[:, s], hh[:, g, q - 1],
                                                ALU.subtract).then_inc(lo_done, 1)
                pool.wait_ge(zve_ready, G + 1)
                nc.gpsimd.tensor_tensor(zr[:, g], zve[:, g], mhalf[:, 0:GT], ALU.pow).then_inc(zr_ready, 1)
                for i in range(GT):
                    Y = GT * G + i
                    pool.wait_ge(w_norm, Y + 1)
                    nc.gpsimd.tensor_tensor(z[:, g, i], z[:, g, i], gam[:, :], ALU.mult).then_inc(pool_g, 1)
                    pool.wait_ge(pool_g, Y + 1)
                    nc.gpsimd.tensor_tensor(z[:, g, i], z[:, g, i], bet[:, :], ALU.add).then_inc(w_affine, 1)

            nc.gpsimd.sem_inc(lo_done, 2)
            schedule(pool, front_stats, nothing, nothing, front_norm, gates, ffn, nothing, nothing)

        @block.scalar
        def _(act):
            def front_tile(n, t):
                act.wait_ge(xn_ready, NT * n + t + 1)
                settle(act)
                nc.scalar.activation(out_sb[:, n, t], xn_st[:, t % 4], ACT.Gelu_apprx_tanh).then_inc(gelu_done, 1)
                act.wait_ge(tx_done, NT * n + t + 1)
                if t == 0:
                    need(act, m2_done, CHUNKS * n)
                nc.scalar.copy(xnT[:, :, 1 + t * P:1 + (t + 1) * P], trX[:, :, :]).then_inc(xe_done, 1)

            def front_norm(n):
                act.wait_ge(gelu_done, NT * n + NT)
                need(act, ss_ready, NT * n)
                for t in range(NT):
                    if t >= 2:
                        act.wait_ge(ss_ready, NT * n + t - 1)
                    settle(act)
                    nc.scalar.activation(junk[:, t % 2], out_sb[:, n, t], ACT.Square,
                                         accum_out=ss[:, t:t + 1]).then_inc(ss_ready, 1)
                need(act, tu_done, NT * n)
                act.wait_ge(rn_ready, n + 1)

            def front_unit(n):
                for t in range(NT):
                    if t >= 2:
                        act.wait_ge(tu_done, NT * n + t - 1)
                    settle(act)
                    nc.scalar.activation(uh_st[:, t % 2], out_sb[:, n, t], ACT.Copy,
                                         scale=rnorm[:, t:t + 1]).then_inc(uh_ready, 1)

            def front_mix(n):
                act.wait_ge(xe_done, NT * n + NT)
                act.wait_ge(weights_ready, 1)
                for c in range(CHUNKS):
                    h, k = divmod(c, KD)
                    need(act, xl_done, CHUNKS * (n - 1) + c + 1 if not isinstance(n, int) or n else 0)
                    nc.scalar.activation(mixt[:, c], xnT[:, k, h * GW:(h + 1) * GW], ACT.Copy,
                                         scale=kmix[:, 0, k:k + 1]).then_inc(m0_done, 1)
                for c in range(CHUNKS):
                    h, k = divmod(c, KD)
                    act.wait_ge(m2_done, CHUNKS * n + c + 1)
                    settle(act)
                    nc.scalar.copy(xmT[:, n, k, h * GW:(h + 1) * GW], mixt[:, c]).then_inc(xh_done, 1)

            def ffn(b, g):
                G = NG * b + g
                act.wait_ge(h_ready, NH * G + 1)
                nc.scalar.activation(sT[M:2 * M, :], hP[(NH * g) % 2][M:2 * M, :], ACT.Tanh,
                                     bias=bo1s[M:2 * M, :], scale=sc[M:2 * M, 8:9]).then_inc(tanh_done, 1)
                act.wait_ge(y_ready, GT * G + GT)

                def mask(q):
                    H = NH * G + q
                    act.wait_ge(maskP_ready, H + 1)
                    act.wait_ge(hm_done, H + 1)
                    s = (NH * g + q) % 2
                    if q == 0:
                        nc.scalar.copy(mask_sb[0:M, s], maskP[0:M, :])
                        nc.scalar.copy(tB[M:2 * M, g], maskP[M:2 * M, :]).then_inc(mask_ready, 1)
                    else:
                        nc.scalar.copy(mask_sb[:, s], maskP[:, :]).then_inc(mask_ready, 1)

                def high(q):
                    H = NH * G + q
                    s = (NH * g + q) % 2
                    act.wait_ge(hm_done, H + 3)
                    if q == 0:
                        nc.scalar.copy(tB[0:M, g], hm[0:M, s])
                        nc.scalar.copy(tA[0:M, g], hm[0:M, s]).then_inc(hi_done, 1)
                    else:
                        nc.scalar.copy(hh[:, g, q - 1], hm[:, s]).then_inc(hi_done, 1)

                act.wait_ge(ohTP_ready, G + 1)
                nc.scalar.copy(ohT[:, :], maskP[0:PAD, :]).then_inc(ohT_ready, 1)
                mask(0)
                for q in range(1, NH):
                    mask(q)
                    high(q - 1)
                high(NH - 1)

            nc.scalar.sem_inc(mask_ready, 1)
            schedule(act, nothing, nothing, front_tile, front_norm, nothing, ffn, front_unit, front_mix)

        @block.vector
        def _(dve):
            count = [0]

            def mark(ins):
                count[0] += 1
                ins.then_inc(dve_setup, 1)

            def link(ins):
                mark(ins)
                dve.wait_ge(dve_setup, count[0])

            ts = nc.vector.tensor_scalar
            stt = nc.vector.scalar_tensor_tensor

            def setup():
                dve.wait_ge(w_loaded, 16 * len(loads))
                dve.wait_ge(consts, 2)
                ts(knobs[:, 1:3], knobs[:, 1:3], -1.0, None, ALU.mult).then_inc(knobs_in, 1)
                mark(nc.vector.tensor_tensor(ema_sq[:, :], ema_row[:, :], ema_row[:, :], ALU.mult))
                link(nc.vector.tensor_reduce(kabs[:, :], kmix[:, :, :].rearrange("p j k -> p k j"), AX.X, ALU.add,
                                             apply_absolute_value=True))
                mark(nc.vector.reduce_sum(ema_n[:, 0:1], ema_sq[:, :], AX.X))
                nc.vector.reduce_max(amax[:, 0:1], kabs[:, :], AX.X)
                for col, src in ((1, w1s[:, :, 0:EM]), (2, w1s[:, :, EM:EM + M]), (3, w2s[:, :, :]),
                                 (4, b1s[:, :]), (5, b2s[:, :])):
                    last = nc.vector.tensor_reduce(amax[:, col:col + 1], src, AX.XY if len(src.shape) == 3 else AX.X, ALU.max,
                                                   apply_absolute_value=True)
                last.then_inc(amax_ready, 1)
                dve.wait_ge(dve_setup, count[0])
                ts(ema_n[:, 0:1], ema_n[:, 0:1], NORM_MIN * NORM_MIN, None, ALU.max).then_inc(ema_ss, 1)
                dve.wait_ge(knobs_exp, 1)
                link(ts(tau[:, 3:5], knobs[:, 1:3], 1.0, None, ALU.add))
                link(nc.vector.reciprocal(tau[:, 5:7], tau[:, 3:5]))
                nc.vector.tensor_copy(tau[:, 1:2], tau[:, 5:6])
                ts(tau[:, 2:3], tau[:, 5:6], -1.0, 1.0, ALU.mult, ALU.add)
                link(ts(tau[:, 7:8], knobs[:, 0:1], -1.0, None, ALU.mult))
                link(nc.vector.tensor_tensor(tau[:, 3:4], tau[:, 6:7], tau[:, 7:8], ALU.mult))
                link(nc.vector.tensor_tensor(tau[:, 4:5], tau[:, 7:8], tau[:, 3:4], ALU.subtract))
                dve.wait_ge(ema_rn, 1)
                link(ts(ema_col[:, :], ema_col[:, :], ema_n[:, 1:2], None, ALU.mult))
                link(nc.vector.tensor_copy(ema_hl[:, :, 0], ema_col[:, :]))
                nc.vector.tensor_tensor(ema_hl[:, :, 1], ema_col[:, :], ema_hl[:, :, 0], ALU.subtract)
                dve.wait_ge(gmax_ready, 1)

                def col(i):
                    return sc[:, i:i + 1]

                link(ts(col(0), gmax[:, 0:1], SCALE_MIN, None, ALU.max))
                link(nc.vector.reciprocal(col(1), col(0)))
                ts(kmix[:, :, :], kmix[:, :, :], col(1), None, ALU.mult)
                link(ts(col(2), gmax[:, 4:5], col(1), SCALE_MIN, ALU.mult, ALU.max))
                link(nc.vector.tensor_tensor(col(2), col(2), gmax[:, 1:2], ALU.max))
                link(nc.vector.reciprocal(col(3), col(2)))
                link(nc.vector.tensor_tensor(col(4), col(2), col(0), ALU.mult))
                link(nc.vector.reciprocal(col(5), col(4)))
                link(ts(col(6), gmax[:, 2:3], SCALE_MIN, None, ALU.max))
                link(nc.vector.reciprocal(col(7), col(6)))
                nc.vector.tensor_tensor(col(8), col(6), col(0), ALU.mult)
                link(ts(col(9), gmax[:, 5:6], col(5), SCALE_MIN, ALU.mult, ALU.max))
                link(nc.vector.tensor_tensor(col(9), col(9), gmax[:, 3:4], ALU.max))
                link(nc.vector.reciprocal(col(10), col(9)))
                link(nc.vector.tensor_tensor(col(11), col(4), col(9), ALU.mult))
                link(nc.vector.reciprocal(col(12), col(11)))
                link(nc.vector.tensor_tensor(col(13), col(12), col(12), ALU.mult))
                link(ts(col(13), col(13), LN_EPS, None, ALU.mult))
                ts(b1s[:, :], b1s[:, :], col(5), None, ALU.mult)
                ts(w1s[:, :, 0:EM], w1s[:, :, 0:EM], col(3), None, ALU.mult)
                ts(w1s[:, :, EM:EM + M], w1s[:, :, EM:EM + M], col(7), None, ALU.mult)
                ts(w2s[:, :, :], w2s[:, :, :], col(10), None, ALU.mult)
                link(ts(b2s[:, :], b2s[:, :], col(12), None, ALU.mult))
                nc.vector.tensor_copy(w1h[:, :, :], w1s[:, :, :])
                nc.vector.tensor_copy(w2h[:, :, :], w2s[:, :, :])
                link(nc.vector.tensor_copy(b2h[:, :], b2s[:, :]))
                nc.vector.tensor_tensor(w1l[:, :, :], w1s[:, :, :], w1h[:, :, :], ALU.subtract)
                nc.vector.tensor_tensor(w2l[:, :, :], w2s[:, 0:NJ, :], w2h[:, 0:NJ, :], ALU.subtract)
                nc.vector.tensor_tensor(tailB[0:M, :], w2s[0:M, NJ, :], w2h[0:M, NJ, :], ALU.subtract)
                nc.vector.tensor_copy(tailB[M:M + PAD, :], b2h[M:M + PAD, :])
                nc.vector.tensor_tensor(tailB[M + PAD:P, :], b2s[M + PAD:P, :], b2h[M + PAD:P, :],
                                        ALU.subtract).then_inc(weights_ready, 1)

            setup_done = [False]

            def front_stats(n):
                dve.wait_ge(x_loaded, 16 * (n + 1))
                for t in range(NT):
                    last = nc.vector.bn_stats(stats[:, t], x_sb[:, n, t])
                last.then_inc(st_ready, 1)
                dve.wait_ge(st_ready, n + 1)
                settle(dve)
                for t in range(NT):
                    last = nc.vector.bn_aggr(mv[:, t], stats[:, t])
                last.then_inc(mv_ready, 1)
                dve.wait_ge(mv_ready, n + 1)
                ts(var_e[:, :], mv[:, :, 1], LN_EPS, None, ALU.add).then_inc(var_ready, 1)
                dve.wait_ge(rstd_ready, n + 1)
                nc.vector.tensor_copy(rstd[:, n], rstd_s[:, :]).then_inc(rstd_kept, 1)
                stt(nbias[:, :], mv[:, :, 0], -1.0, rstd_s[:, :], ALU.mult, ALU.mult).then_inc(nb_ready, 1)
                dve.wait_ge(nb_ready, n + 1)
                if not setup_done[0]:
                    setup_done[0] = True
                    setup()

            def front_tile(n, t):
                need(dve, tx_done, NT * n + t - 3)
                need(dve, gelu_done, NT * n + t - 3)
                ts(xn_st[:, t % 4], x_sb[:, n, t], rstd_s[:, t:t + 1], nbias[:, t:t + 1],
                   ALU.mult, ALU.add).then_inc(xn_ready, 1)

            def front_norm(n):
                dve.wait_ge(ss_ready, NT * n + NT)
                ts(ss_b[:, :], ss[:, :], NORM_MIN * NORM_MIN, None, ALU.max).then_inc(ss_bounded, 1)

            def front_unit(n):
                dve.wait_ge(rn_ready, n + 1)

                def split(t):
                    dve.wait_ge(uh_ready, NT * n + t + 1)
                    stt(ul_st[:, t % 2], out_sb[:, n, t], rnorm[:, t:t + 1], uh_st[:, t % 2],
                        ALU.mult, ALU.subtract).then_inc(ul_ready, 1)

                def keep(t):
                    dve.wait_ge(tu_done, NT * n + t + 1)
                    nc.vector.tensor_copy(uT[:, n, :, t * P:(t + 1) * P], trU).then_inc(ue_done, 1)

                split(0)
                for t in range(1, NT):
                    split(t)
                    keep(t - 1)
                keep(NT - 1)

            def front_mix(n):
                for c in range(CHUNKS):
                    h, k = divmod(c, KD)
                    dve.wait_ge(m0_done, CHUNKS * n + c + 1)
                    stt(mixt[:, c], xnT[:, k, 1 + h * GW:1 + (h + 1) * GW], kmix[:, 1, k:k + 1], mixt[:, c],
                        ALU.mult, ALU.add).then_inc(m1_done, 1)
                for c in range(CHUNKS):
                    h, k = divmod(c, KD)
                    dve.wait_ge(m1_done, CHUNKS * n + c + 1)
                    stt(mixt[:, c], xnT[:, k, 2 + h * GW:2 + (h + 1) * GW], kmix[:, 2, k:k + 1], mixt[:, c],
                        ALU.mult, ALU.add).then_inc(m2_done, 1)
                for c in range(CHUNKS):
                    h, k = divmod(c, KD)
                    dve.wait_ge(xh_done, CHUNKS * n + c + 1)
                    nc.vector.tensor_tensor(xmT[:, n, KD + k, h * GW:(h + 1) * GW], mixt[:, c],
                                            xmT[:, n, k, h * GW:(h + 1) * GW],
                                            ALU.subtract).then_inc(xl_done, 1)

            def sim(b, t):
                for q, (tt, lo, hi) in enumerate(PIECES):
                    if tt == t:
                        dve.wait_ge(sim_ready, NP * b + q + 1)
                        nc.vector.reduce_max(smax[:, t, lo // 4:lo // 4 + 1], simP[q % 2][:, 0:(hi - lo) * P],
                                             AX.X).then_inc(sim_free, 1)

            def gates(b):
                n = [0]

                def chain(ins):
                    n[0] += 1
                    ins.then_inc(fam_c, 1)
                    dve.wait_ge(fam_c, 5 * b + n[0])

                dve.wait_ge(sim_free, NP * b + NP + 2)
                chain(nc.vector.tensor_tensor(seq[:, :], smax[:, :, 0], smax[:, :, 1], ALU.max))
                dve.wait_ge(ema_ready, b + 1)
                chain(nc.vector.reduce_sum(ems[:, :], emaP, AX.X))
                chain(ts(fix[:, :], ems[:, 0:1], first_row[:, :], None, ALU.mult))
                chain(stt(seq[:, 0:1], seq[:, 0:1], not_first[:, :], fix[:, :], ALU.mult, ALU.add))
                chain(ts(expo[:, :], seq[:, :], tau[:, 3:4], None, ALU.mult))
                stt(expo[:, :], ems[:, :], tau[:, 4:5], expo[:, :], ALU.mult, ALU.add).then_inc(expo_ready, 1)
                dve.wait_ge(nov_ready, b + 1)
                ts(gate[:, :], novelty[:, :], tau[:, 1:2], tau[:, 2:3], ALU.mult, ALU.add).then_inc(gate_ready, 1)

            def ffn(b, g):
                G = NG * b + g
                n = [0]

                def chain(ins):
                    n[0] += 1
                    ins.then_inc(arg_c, 1)
                    dve.wait_ge(arg_c, 5 * G + n[0])

                def over(v):
                    return v.to_broadcast([P, GT, E])

                dve.wait_ge(sco_ready, G + 1)
                chain(nc.vector.tensor_tensor(sco[:, :, :], scoP, bo2r[:, :].unsqueeze(1).to_broadcast([P, GT, E]),
                                              ALU.add))
                chain(nc.vector.reduce_max(top[:, :, 0], sco[:, :, :], AX.X))
                chain(nc.vector.tensor_tensor(sco[:, :, :], sco[:, :, :], over(top[:, :, 0:1]), ALU.is_ge))
                chain(nc.vector.tensor_tensor(sco[:, :, :], sco[:, :, :], prio[:, :, :], ALU.mult))
                chain(nc.vector.reduce_max(top[:, :, 1], sco[:, :, :], AX.X))
                nc.vector.tensor_tensor(ohp[:, :, 0:E], sco[:, :, :], over(top[:, :, 1:2]),
                                        ALU.is_equal).then_inc(oh_ready, 1)
                for q in range(NH):
                    H = NH * G + q
                    s = (NH * g + q) % 2
                    r = M if q == 0 else P
                    dve.wait_ge(h_ready, H + 1)
                    dve.wait_ge(mask_ready, H + 2)
                    dve.wait_ge(lo_done, H + 1)
                    bias = b1s[0:M, NJ:NJ + 1] if q == 0 else b1s[:, q - 1:q]
                    stt(hm[0:r, s], hP[s][0:r, :], bias, mask_sb[0:r, s], ALU.add, ALU.mult).then_inc(hm_done, 1)
                dve.wait_ge(rstd_kept, b + 1)
                ts(rc[:, g], rstd[:, b, g * GT:(g + 1) * GT], sc[:, 12:13], None, ALU.mult).then_inc(zs_c, 1)
                dve.wait_ge(zs_c, 2 * G + 1)
                for i in range(GT):
                    Y = GT * G + i
                    dve.wait_ge(y_ready, Y + 1 + 2 * GT)
                    stt(z[:, g, i], x_sb[:, b, g * GT + i], rc[:, g, i:i + 1], yP[:, :], ALU.mult,
                        ALU.add).then_inc(z_done, 1)
                dve.wait_ge(z_done, GT * G + GT + 2)
                for i in range(GT):
                    last = nc.vector.bn_stats(zst[:, i], z[:, g, i])
                last.then_inc(zs_c, 1)
                dve.wait_ge(zs_c, 2 * G + 2)
                dve.wait_ge(gate_ready, b + 1)
                for i in range(GT):
                    t = g * GT + i
                    stt(out_sb[:, b, t], out_sb[:, b, t], gate[:, t:t + 1], x_sb[:, b, t],
                        ALU.mult, ALU.add).then_inc(a_done, 1)
                for i in range(GT):
                    last = nc.vector.bn_aggr(zmv[:, g, i], zst[:, i])
                last.then_inc(zmv_ready, 1)
                dve.wait_ge(zmv_ready, G + 1)
                ts(zve[:, g], zmv[:, g, :, 1], sc[:, 13:14], None, ALU.add).then_inc(zve_ready, 1)
                dve.wait_ge(zr_ready, G + 1)
                stt(zb[:, g], zmv[:, g, :, 0], -1.0, zr[:, g], ALU.mult, ALU.mult).then_inc(zb_ready, 1)
                dve.wait_ge(zb_ready, G + 1)
                for i in range(GT):
                    ts(z[:, g, i], z[:, g, i], zr[:, g, i:i + 1], zb[:, g, i:i + 1],
                       ALU.mult, ALU.add).then_inc(w_norm, 1)
                for i in range(GT):
                    Y = GT * G + i
                    dve.wait_ge(w_affine, Y + 1)
                    dve.wait_ge(a_done, Y + 1)
                    t = g * GT + i
                    last = nc.vector.tensor_tensor(out_sb[:, b, t], out_sb[:, b, t], z[:, g, i], ALU.add)
                last.then_inc(o_ready, 1)

            nc.vector.sem_inc(sim_free, 2)
            nc.vector.sem_inc(expo_ready, 1)
            nc.vector.sem_inc(hm_done, 2)
            nc.vector.sem_inc(z_done, 2)
            schedule(dve, front_stats, sim, front_tile, front_norm, gates, ffn, front_unit, front_mix)

        @block.tensor
        def _(pe):
            mm = nc.tensor.matmul

            def front_tile(n, t):
                if isinstance(n, int) and n == 0 and t == 0:
                    pe.wait_ge(consts, 2)
                pe.wait_ge(xn_ready, NT * n + t + 1)
                need(pe, xe_done, NT * n + t)
                if t == 0:
                    need(pe, ue_done, NT * n)
                for k in range(KD):
                    last = nc.tensor.transpose(trX[:, k], xn_st[:, t % 4, k * P:(k + 1) * P], ident[:, :])
                last.then_inc(tx_done, 1)

            def front_unit(n):
                pe.wait_ge(xe_done, NT * n + NT)
                for t in range(NT):
                    pe.wait_ge(ul_ready, NT * n + t + 1)
                    need(pe, ue_done, NT * n + t)
                    for part, st in enumerate((uh_st, ul_st)):
                        for k in range(KD):
                            last = nc.tensor.transpose(trU[:, part * KD + k], st[:, t % 2, k * P:(k + 1) * P],
                                                       ident16[:, :])
                    last.then_inc(tu_done, 1)

            PAIRS = ((0, 0), (0, 1), (1, 0))

            def sim(b, t):
                if t == 0:
                    pe.wait_ge(ue_done, NT * b + NT)
                for q, (tt, lo, hi) in enumerate(PIECES):
                    if tt != t:
                        continue
                    pe.wait_ge(sim_free, NP * b + q + 1)
                    w = (hi - lo) * P
                    bank = simP[q % 2]
                    steps = [(i, j, k) for i, j in PAIRS for k in range(KD)]
                    for n, (i, j, k) in enumerate(steps):
                        last = mm(bank[:, 0:w], uT[:, b, i * KD + k, t * P:(t + 1) * P],
                                  uT[:, b, j * KD + k, lo * P:hi * P], start=(n == 0), stop=(n == len(steps) - 1))
                        if n == 0 and hi == t + 1:
                            mm(bank[:, w - P:w], ident16[:, :], future16[:, :], start=False, stop=False)
                    last.then_inc(sim_ready, 1)
                if t == 0:
                    pe.wait_ge(expo_ready, b + 1)
                    pe.wait_ge(weights_ready, 1)
                for n, (i, k) in enumerate((i, k) for i in range(2) for k in range(KD)):
                    last = mm(emaP[:, t], uT[:, b, i * KD + k, t * P:(t + 1) * P], ema_hl[:, k, :],
                              start=(n == 0), stop=(n == 2 * KD - 1))
                if t == NT - 1:
                    last.then_inc(ema_ready, 1)

            def ffn(b, g):
                G = NG * b + g
                tok = slice(g * GW, (g + 1) * GW)

                def hidden(q):
                    H = NH * G + q
                    pe.wait_ge(hm_done, H + 1)
                    cols = slice(NJ * 2 * M, NJ * 2 * M + P) if q == 0 else slice((q - 1) * P, q * P)
                    steps = [(i, j, k) for i, j in PAIRS for k in range(KD)]
                    for n, (i, j, k) in enumerate(steps):
                        last = mm(hP[(NH * g + q) % 2][:, :], (w1h, w1l)[i][:, k, cols],
                                  xmT[:, b, j * KD + k, tok], start=(n == 0), stop=(n == len(steps) - 1))
                    last.then_inc(h_ready, 1)

                def masks(q):
                    H = NH * G + q
                    pe.wait_ge(mask_ready, H + 1)
                    if q == 0:
                        pe.wait_ge(ohT_ready, G + 1)
                    mm(maskP[:, :], pick[:, q, :], ohT[:, :], start=True,
                       stop=True).then_inc(maskP_ready, 1)

                pe.wait_ge(xl_done, CHUNKS * b + KD * (g + 1))
                hidden(0)
                hidden(1)
                pe.wait_ge(tanh_done, G + 1)
                if g == 0:
                    pe.wait_ge(expo_ready, b + 2)
                for i in range(GT):
                    last = mm(scoP[:, i], sT[M:2 * M, i * P:(i + 1) * P], wo2s[M:2 * M, :], start=True, stop=True)
                last.then_inc(sco_ready, 1)
                pe.wait_ge(oh_ready, G + 1)
                pe.wait_ge(mask_ready, NH * G + 1)
                for i in range(GT):
                    last = mm(maskP[0:PAD, i * P:(i + 1) * P], ohp[:, i, :], ident16[:, :], start=True, stop=True)
                last.then_inc(ohTP_ready, 1)
                masks(0)
                masks(1)
                for q in range(2, NH):
                    hidden(q)
                    masks(q)
                for i in range(GT):
                    Y = GT * G + i
                    pe.wait_ge(z_done, Y + 2)
                    if i == 0:
                        pe.wait_ge(lo_done, 2 + NH * (G + 1))
                    cols = slice(i * P, (i + 1) * P)
                    mm(yP[:, :], tA[:, g, cols], w2h[:, NJ], start=True, stop=False)
                    mm(yP[:, :], tB[:, g, cols], tailB[:, :], start=False, stop=False)
                    for j in range(NJ):
                        mm(yP[:, :], hh[:, g, j, cols], w2h[:, j], start=False, stop=False)
                        mm(yP[:, :], hl[:, g, j, cols], w2h[:, j], start=False, stop=False)
                        last = mm(yP[:, :], hh[:, g, j, cols], w2l[:, j], start=False, stop=(j == NJ - 1))
                    last.then_inc(y_ready, 1)

            pe.sem_inc(y_ready, 2 * GT)
            schedule(pe, nothing, sim, front_tile, nothing, nothing, ffn, front_unit, nothing)


_INS = ["L0_attn_x", "L0_attn_ema_out", "L0_attn_log_tau", "L0_attn_log_blend", "L0_attn_logit_blend_seq",
        "L0_ffn_mix_kernel", "L0_ffn_W1", "L0_ffn_b1", "L0_ffn_W2", "L0_ffn_b2", "L0_ffn_Wo1", "L0_ffn_bo1",
        "L0_ffn_Wo2", "L0_ffn_bo2", "L0_ffn_gamma", "L0_ffn_beta"]


def kernel(**inputs):
    import numpy as _np
    import concourse.bacc as _bacc
    from concourse import mybir as _mybir
    from concourse.bass_utils import run_bass_kernel_spmd as _run

    nc = _bacc.Bacc("TRN2", target_bir_lowering=False, num_devices=1)
    arrays, args = {}, []
    for name in _INS:
        a = _np.ascontiguousarray(inputs[name])
        if a.ndim == 0:
            a = a.reshape(1)
        arrays[f"in_{name}"] = a
        args.append(nc.dram_tensor(f"in_{name}", a.shape, _mybir.dt.from_np(a.dtype), kind="ExternalInput").ap())
    shape = arrays["in_L0_attn_x"].shape
    out = nc.dram_tensor("out_0", shape, _mybir.dt.float32, kind="ExternalOutput").ap()
    build(nc, *args, out)
    r = _run(nc, [arrays], core_ids=[0])
    return r.results[0]["out_0"]
```

```python
from contextlib import ExitStack

import concourse.bass as bass
from concourse import mybir

F32 = mybir.dt.float32
F16 = mybir.dt.float16
ALU = mybir.AluOpType
ACT = mybir.ActivationFunctionType
AX = mybir.AxisListType
RMAX = bass.bass_isa.ReduceOp.max

P = 128
LN_EPS = 1e-5
NORM_MIN = 1e-12
SCALE_MIN = 1e-4
NATURAL = 2.718281828459045


PLAN = dict(
    row_stats=(-15.35, 0.4), variance=(-12.2, 0), invert=(-10.9, 0), shift=(-10, 0), norm=(-9, 0.45),
    transpose=(-8, 0.45), gelu=(-7.8, 0.35), square=(-7.7, 0.4), keep_x=(-7.95, 0.45), bound_ss=(-4.8, 0),
    invert_ss=(-4.6, 0), tap0=(-6.05, 0.85), tap1=(-5.25, 0.85), tap2=(-4.95, 0.85), mix_hi=(-4.25, 0.75),
    mix_lo=(-4.75, 1.05), unit_hi=(-3.2, 0.35), unit_lo=(-2.9, 0.4), unit_turn=(-2.4, 0.45),
    keep_u=(-2.35, 0.45),
    inv=(0.95, 0), ema_dot=(2, 0), ema_sum=(1.9, 0), sim=(0.15, 0.65), sim_max=(0.75, 0.65), familiar=(8.7, 0),
    exponent=(8, 0), gate=(9.5, 0),
    router=(-1.75, 0), tanh=(-1.6, 0), keep_h8=(-0.9, 0), scores=(-1.4, 0), argmax=(-1.15, 0), pick=(-0.95, 0),
    keep_pick=(-1, 0), mask=(-0.55, 0.6), keep_mask=(-0.55, 0.65), hidden=(-0.7, 0.8), masked=(-0.4, 0.8),
    high=(-0.1, 0.75), low=(0, 0.65), low8=(0.35, 0), expert=(3.65, 0.8), residual=(3.9, 0.75),
    z_stats=(4.15, 0.85), z_var=(7.2, 0), z_invert=(6.95, 0), z_shift=(7.65, 0), affine=(8.9, 0.05),
    times_gamma=(8.4, 0.05), plus_beta=(9.6, 0.15), gated=(9.5, 0.45), final=(10.5, 0.85),
    ema_norm=(-12.75, 0), tap_max=(-12.5, 0), tap_scale=(-9.3, 0), constants=(-9.25, 0), w_max=(-11.9, 0),
    w_scale=(-8.55, 0), w1_high=(-8.05, 0), w1_low=(-7.15, 0), w2_high=(-5.7, 0), w2_low=(-2.25, 0),
)
FIRST = dict(
    PLAN,
    row_stats=(-21, 0.1), variance=(-18.25, 0), invert=(-13, 0), shift=(-18.1, 0), norm=(-13.45, 0.15),
    transpose=(-14.85, 0.15), gelu=(-14.1, 0.05), square=(-14.05, 0.25), keep_x=(-14.1, 0.3),
    bound_ss=(-8.6, 0), invert_ss=(-11.65, 0), tap0=(-11.9, 0.25), tap1=(-9.2, 0.3), tap2=(-8.85, 0.4),
    mix_hi=(-7.7, 0.15), mix_lo=(-9.15, 0.5), unit_hi=(-8.8, 0.4), unit_lo=(-8.25, 0.55),
    unit_turn=(-11.3, 0.25), keep_u=(-7.7, 0.45),
    inv=(-1.9, 0), ema_dot=(0.1, 0), ema_sum=(0.3, 0), sim=(-2.4, 0.6), sim_max=(-2.05, 0.6),
    familiar=(7.25, 0), exponent=(7, 0), gate=(7.65, 0),
    router=(-5.05, 0), tanh=(-2.95, 0), keep_h8=(-1, 0), scores=(-1.7, 0), argmax=(-1.2, 0), pick=(-0.75, 0),
    keep_pick=(-0.5, 0), mask=(-0.3, 0.4), keep_mask=(-0.5, 0.55), hidden=(-0.3, 0.6), masked=(-0.1, 0.7),
    high=(-0.1, 0.7), low=(-1.1, 0.85), low8=(1.8, 0), expert=(3.15, 0.7), residual=(3.5, 0.7),
    z_stats=(5, 0.55), z_var=(7.7, 0), z_invert=(8.15, 0), z_shift=(8.45, 0), affine=(8.85, 0.35),
    times_gamma=(8.15, 0.3), plus_beta=(9.15, 0.25), gated=(8.45, 0.25), final=(10.95, 0.05),
)
LAST = dict(
    PLAN,
    row_stats=(-15.85, 0.25), variance=(-13.75, 0), invert=(-11.3, 0), shift=(-10.05, 0), norm=(-8.45, 0.45),
    transpose=(-8.1, 0.45), gelu=(-8.1, 0.4), square=(-7.85, 0.5), keep_x=(-8.05, 0.45), bound_ss=(-4, 0),
    invert_ss=(-4, 0), tap0=(-5.95, 0.8), tap1=(-5, 0.65), tap2=(-4.75, 0.9), mix_hi=(-3.95, 0.65),
    mix_lo=(-4.8, 1.3), unit_hi=(-3.35, 0.35), unit_lo=(-2.45, 0.35), unit_turn=(-2.05, 0.35),
    keep_u=(-1.9, 0.3),
    ema_dot=(1.85, 0), ema_sum=(2.45, 0), sim=(0.65, 0.6), sim_max=(1.05, 0.6), familiar=(7.85, 0),
    gate=(9.45, 0),
    router=(-4.1, 0), tanh=(-4.5, 0), keep_h8=(-4.4, 0), scores=(-3.05, 0), argmax=(-3.25, 0), pick=(-2.2, 0),
    keep_pick=(-2.5, 0), mask=(-1.65, 0.7), keep_mask=(-0.45, 0.6), hidden=(-1.35, 0.8), masked=(-0.4, 0.45),
    high=(-0.1, 0.85), low=(0, 0.6), low8=(0.05, 0), expert=(3.05, 1.2), residual=(3.35, 0.85),
    z_stats=(3.4, 1), z_var=(6.65, 0), z_invert=(11.7, 0), z_shift=(10.45, 0), affine=(17.6, 1.5),
    times_gamma=(13.6, 1.5), plus_beta=(16.95, 1.6), gated=(11.15, 0.4), final=(23.5, 1.75),
)
SETUP = ("ema_norm", "tap_max", "tap_scale", "constants", "w_max", "w_scale", "w1_high", "w1_low", "w2_high",
         "w2_low")
FRONT = ("row_stats", "variance", "invert", "shift", "norm", "transpose", "gelu", "square", "keep_x", "bound_ss",
         "invert_ss", "tap0", "tap1", "tap2", "mix_hi", "mix_lo", "unit_hi", "unit_lo", "unit_turn", "keep_u")
SIM = ("inv", "ema_dot", "ema_sum", "sim", "sim_max", "familiar", "exponent", "gate")
BATCH_STEPS = dict(row_stats="tiles", norm="tiles", transpose="tiles", gelu="tiles", square="tiles", keep_x="tiles",
                   tap0="chunks", tap1="chunks", tap2="chunks", mix_hi="chunks", mix_lo="chunks", unit_hi="tiles",
                   unit_lo="tiles", unit_turn="tiles", keep_u="tiles", sim="pieces", sim_max="pieces")
GROUP_STEPS = dict(mask="blocks", keep_mask="blocks", hidden="pairs", masked="blocks", high="blocks", low="pairs",
                   expert="rows", residual="rows", z_stats="rows", affine="rows", times_gamma="rows",
                   plus_beta="rows", gated="rows", final="rows")


def order(names, batches, groups, counts):
    at = []
    for name in names:
        if name in SETUP:
            at.append((PLAN[name][0], name, ()))
        elif name in FRONT or name in SIM:
            for b in range(batches):
                start, step = (FIRST if b == 0 else LAST if b == batches - 1 else PLAN)[name]
                n = counts[BATCH_STEPS[name]] if name in BATCH_STEPS else 0
                at += [(8 * b + start + step * i, name, (b, i)) for i in range(n)] or [(8 * b + start, name, (b,))]
        else:
            for G in range(groups * batches):
                start, step = (LAST if G == groups * batches - 1 else FIRST if G == 0 else PLAN)[name]
                n = counts[GROUP_STEPS[name]] if name in GROUP_STEPS else 0
                first = 1 if name in ("hidden", "low") else 0
                at += [(8 / groups * G + start + step * i, name, (G, i)) for i in range(first, n)] or \
                    [(8 / groups * G + start, name, (G,))]
    at.sort(key=lambda entry: entry[0])
    return [(name, *args) for _, name, args in at]


def build(nc, x, ema, log_tau, log_blend, logit_seq, mix_k, W1, b1, W2, b2, Wo1, bo1, Wo2, bo2,
          gamma, beta, out):
    B, T, D = x.shape
    E, _, M = W1.shape
    NT = T // P
    KD = D // P
    GT = 4
    NG = NT // GT
    GW = GT * P
    NJ = E // 2
    NH = NJ + 1
    EM = E * M
    PAD = 32
    CHUNKS = NG * KD
    PIECES = [(t, 0, min(t + 1, 4)) for t in range(4)]
    PIECES += [p for t in range(4, NT) for p in ((t, 0, 4), (t, 4, t + 1))]
    NP = len(PIECES)
    PAIRS = ((0, 0), (0, 1), (1, 0))

    COUNTS = dict(tiles=NT, chunks=CHUNKS, pieces=NP, rows=GT, blocks=NH, pairs=NH)

    def in_order(names):
        return order(names, B, NG, COUNTS)

    HIDDEN = in_order(("router", "hidden"))
    SHORT = in_order(("transpose", "unit_turn", "scores", "ema_dot", "pick", "mask"))
    STORES = in_order(("final",))

    ctx = ExitStack()
    with ctx:
        def sb(name, shape, dt=F32):
            return ctx.enter_context(nc.sbuf_tensor(name, shape, dt))

        def ps(name, shape, dt=F32):
            return ctx.enter_context(nc.psum_tensor(name, shape, dt))

        def sem(name):
            return ctx.enter_context(nc.semaphore(name))

        ident = sb("ident", [P, P])
        ident16 = sb("ident16", [P, P], F16)
        future16 = sb("future16", [P, P], F16)
        prio = sb("prio", [P, GT, E])
        pick = sb("pick", [PAD, NH, P], F16)
        mhalf = sb("mhalf", [P, NT])
        e_base = sb("e_base", [P, NT])
        first_row = sb("first_row", [P, 1])
        not_first = sb("not_first", [P, 1])
        knobs = sb("knobs", [P, 3])
        knobs_e = sb("knobs_e", [P, 3])
        tau = sb("tau", [P, 8])
        kmix = sb("kmix", [P, 3, KD])
        kmix_s = sb("kmix_s", [P, 3, KD])
        kabs = sb("kabs", [P, KD])
        ema_row = sb("ema_row", [P, D])
        ema_sq = sb("ema_sq", [P, D])
        ema_n = sb("ema_n", [P, 2])
        ema_col = sb("ema_col", [P, KD])
        ema_hl = sb("ema_hl", [P, KD, 2], F16)
        w1s = sb("w1s", [P, KD, EM + M])
        w1h = sb("w1h", [P, KD, EM + M], F16)
        w1l = sb("w1l", [P, KD, EM + M], F16)
        w2s = sb("w2s", [P, NJ + 1, D])
        w2h = sb("w2h", [P, NJ + 1, D], F16)
        w2l = sb("w2l", [P, NJ, D], F16)
        b2s = sb("b2s", [P, D])
        tailB = sb("tailB", [P, D], F16)
        b2h = sb("b2h", [P, D], F16)
        b1s = sb("b1s", [P, NJ + 1])
        b1n = sb("b1n", [P, NJ + 1])
        bo1s = sb("bo1s", [P, 1])
        wo2s = sb("wo2s", [P, E])
        bo2r = sb("bo2r", [P, E])
        gam = sb("gam", [P, D])
        bet = sb("bet", [P, D])
        amax = sb("amax", [P, 6])
        gmax = sb("gmax", [P, 6])
        sc = sb("sc", [P, 24])

        x_sb = sb("x_sb", [P, B, NT, D])
        out_sb = sb("out_sb", [P, B, NT, D])
        rstd = sb("rstd", [P, B, NT])
        gate = sb("gate", [P, B, NT])
        inv = sb("inv", [P, B, NT])

        uT = sb("uT", [P, 2, 2 * KD, T], F16)
        xmT = sb("xmT", [P, 2, 2 * KD, T], F16)

        stats = sb("stats", [P, NT, 6])
        mv = sb("mv", [P, NT, 2])
        var_e = sb("var_e", [P, NT])
        nbias = sb("nbias", [P, 2, NT])
        ss = sb("ss", [P, NT])
        ss_b = sb("ss_b", [P, NT])
        rnorm = sb("rnorm", [P, 2, NT])
        xn_st = sb("xn_st", [P, 4, D])
        junk = sb("junk", [P, 2, D])
        uh_st = sb("uh_st", [P, 4, D], F16)
        ul_st = sb("ul_st", [P, 4, D], F16)
        xnT = sb("xnT", [P, KD, T + 2])
        mixt = sb("mixt", [P, CHUNKS, GW])

        smax = sb("smax", [P, NT, 2])
        seq = sb("seq", [P, NT])
        ems = sb("ems", [P, NT])
        fix = sb("fix", [P, 1])
        expo = sb("expo", [P, NT])
        novelty = sb("novelty", [P, NT])

        sT = sb("sT", [P, GW])
        h8 = sb("h8", [M, GW])
        sco = sb("sco", [P, GT, E])
        top = sb("top", [P, GT, 2])
        ohp = sb("ohp", [P, GT, PAD], F16)
        ohT = sb("ohT", [PAD, 2, GW], F16)
        mask_sb = sb("mask_sb", [P, 4, GW], F16)
        hm = sb("hm", [P, 4, GW])
        hh = sb("hh", [P, NG, NJ, GW], F16)
        hl = sb("hl", [P, NG, NJ, GW], F16)
        tA = sb("tA", [P, NG, GW], F16)
        tB = sb("tB", [P, NG, GW], F16)
        z = sb("z", [P, NG, GT, D])
        zst = sb("zst", [P, GT, 6])
        zmv = sb("zmv", [P, NG, GT, 2])
        zve = sb("zve", [P, NG, GT])
        zr = sb("zr", [P, NG, GT])
        zb = sb("zb", [P, NG, GT])

        simP = [ps(f"simP{i}", [P, 512]) for i in range(2)]
        hP = [ps(f"hP{i}", [P, GW]) for i in range(2)]
        yP = ps("yP", [P, D])
        shortP = [ps(f"shortP{i}", [P, 512]) for i in range(3)]

        def short(*use):
            return shortP[SHORT.index(use) % 3]

        def rows_in(bank):
            return bank[:, 0:KD * P].rearrange("p (k q) -> p k q", k=KD)

        def units_in(bank):
            return bank[:, 0:KD * P].bitcast(F16).rearrange("p (c q) -> p c q", c=2 * KD)

        def scores_in(bank):
            return bank[:, 0:GT * E].rearrange("p (i e) -> p i e", i=GT)

        def ema_in(bank):
            return bank[:, 0:2 * NT].rearrange("p (t c) -> p t c", c=2)

        padded = sem("padded")
        small_loaded = sem("small_loaded")
        w1_loaded = sem("w1_loaded")
        w2_loaded = sem("w2_loaded")
        result_ready = sem("result_ready")
        stored = sem("stored")
        blank = sem("blank")
        consts = sem("consts")
        var_ready = sem("var_ready")
        rstd_ready = sem("rstd_ready")
        knobs_in = sem("knobs_in")
        knobs_exp = sem("knobs_exp")
        ema_ss = sem("ema_ss")
        ema_rn = sem("ema_rn")
        tap_amax = sem("tap_amax")
        tap_gmax = sem("tap_gmax")
        amax_ready = sem("amax_ready")
        gmax_ready = sem("gmax_ready")
        ss_bounded = sem("ss_bounded")
        rn_ready = sem("rn_ready")
        xh_done = sem("xh_done")
        xl_done = sem("xl_done")
        expo_ready = sem("expo_ready")
        nov_ready = sem("nov_ready")
        hi_done = sem("hi_done")
        lo_done = sem("lo_done")
        zve_ready = sem("zve_ready")
        zr_ready = sem("zr_ready")
        w_norm = sem("w_norm")
        w_gamma = sem("w_gamma")
        w_affine = sem("w_affine")
        scales_ready = sem("scales_ready")
        w1_split = sem("w1_split")
        w2_split = sem("w2_split")
        gelu_done = sem("gelu_done")
        ss_ready = sem("ss_ready")
        xn_ready = sem("xn_ready")
        tx_done = sem("tx_done")
        m2_done = sem("m2_done")
        xe_done = sem("xe_done")
        tu_done = sem("tu_done")
        uh_ready = sem("uh_ready")
        h_ready = sem("h_ready")
        sim_ready = sem("sim_ready")
        ue_done = sem("ue_done")
        taps_ready = sem("taps_ready")
        m0_done = sem("m0_done")
        sco_ready = sem("sco_ready")
        tanh_done = sem("tanh_done")
        hm_done = sem("hm_done")
        h8_done = sem("h8_done")
        ohTP_ready = sem("ohTP_ready")
        ohT_ready = sem("ohT_ready")
        maskP_ready = sem("maskP_ready")
        y_ready = sem("y_ready")
        mask_ready = sem("mask_ready")
        zb_ready = sem("zb_ready")
        own_setup = sem("own_setup")
        ema_split = sem("ema_split")
        w1_ready = sem("w1_ready")
        w2_ready = sem("w2_ready")
        st_ready = sem("st_ready")
        mv_ready = sem("mv_ready")
        nb_ready = sem("nb_ready")
        ul_ready = sem("ul_ready")
        m1_done = sem("m1_done")
        inv_ready = sem("inv_ready")
        ema_ready = sem("ema_ready")
        ems_ready = sem("ems_ready")
        sim_free = sem("sim_free")
        own_gate = sem("own_gate")
        gate_ready = sem("gate_ready")
        own_argmax = sem("own_argmax")
        oh_ready = sem("oh_ready")
        lo8_done = sem("lo8_done")
        z_done = sem("z_done")
        zst_ready = sem("zst_ready")
        zmv_ready = sem("zmv_ready")
        gated = sem("gated")
        x0_loaded = [sem(f"x0_loaded{g}") for g in range(NG)]
        x_loaded = [sem(f"x_loaded{n}") for n in range(1, B)]

        def need(eng, s, v):
            if v > 0:
                eng.wait_ge(s, v)

        def run(parts):
            for name, *args in in_order(tuple(parts)):
                parts[name](*args)

        small_loads = [
            (kmix[:, :, k], mix_k[:, k * P:(k + 1) * P].rearrange("j p -> p j")) for k in range(KD)
        ] + [
            (knobs[:, 0:1], log_tau.partition_broadcast(P)),
            (knobs[:, 1:2], log_blend.partition_broadcast(P)),
            (knobs[:, 2:3], logit_seq.partition_broadcast(P)),
            (ema_row[:, :], ema.partition_broadcast(P)),
            (ema_col[:, :], ema.rearrange("(k p) -> p k", p=P)),
        ]
        w1_loads = []
        for k in range(KD):
            w1_loads += [
                (w1s[:, k, 0:EM].rearrange("p (e m) -> p e m", e=E),
                 W1[:, k * P:(k + 1) * P, :].rearrange("e p m -> p e m")),
                (w1s[:, k, EM:EM + M], Wo1[k * P:(k + 1) * P, :]),
            ]
        w2_loads = [
            (b1s[:, 0:NJ], b1[0:2 * NJ, :].rearrange("(j a) m -> (a m) j", a=2)),
            (b1s[0:M, NJ:NJ + 1], b1[E - 1:E, :].rearrange("o m -> m o")),
            (w2s[:, 0:NJ, :], W2[0:2 * NJ].rearrange("(j a) m d -> (a m) j d", a=2)),
            (w2s[0:M, NJ, :], W2[E - 1]),
            (w2s[M:2 * M, NJ, :], W2[E - 1]),
            (b2s[M:M + E, :], b2),
            (b2s[M + PAD:M + PAD + E, :], b2),
            (bo1s[M:2 * M, :], bo1.rearrange("(m o) -> m o", o=1)),
            (wo2s[M:2 * M, :], Wo2),
            (bo2r[:, :], bo2.partition_broadcast(P)),
            (gam[:, :], gamma.partition_broadcast(P)),
            (bet[:, :], beta.partition_broadcast(P)),
        ]

        block = ctx.enter_context(nc.Block())

        @block.sync
        def _(sp):
            xv = x.rearrange("b (t p) d -> b p t d", p=P)
            for g in range(NG):
                sp.dma_start(x_sb[:, 0, g * GT:(g + 1) * GT], xv[0, :, g * GT:(g + 1) * GT]).then_inc(x0_loaded[g], 16)
            for dst, src in small_loads:
                sp.dma_start(dst, src, allow_slow_non_contiguous=True).then_inc(small_loaded, 16)
            for dst, src in w1_loads:
                sp.dma_start(dst, src).then_inc(w1_loaded, 16)
            sp.wait_ge(padded, 1)
            for dst, src in w2_loads:
                sp.dma_start(dst, src, allow_slow_non_contiguous=True).then_inc(w2_loaded, 16)
            for n in range(1, B):
                sp.dma_start(x_sb[:, n], xv[n]).then_inc(x_loaded[n - 1], 16)

            ov = out.rearrange("b (t p) d -> b p t d", p=P)

            def final(G, i):
                b, g = divmod(G, NG)
                t = g * GT + i
                if i % 2:
                    sp.wait_ge(result_ready, GT * G + i + 1)
                    sp.dma_start(ov[b, :, t - 1:t + 1], out_sb[:, b, t - 1:t + 1]).then_inc(stored, 16)

            for _, G, i in STORES:
                final(G, i)
            sp.wait_ge(stored, 16 * NG * B * GT // 2)

        @block.gpsimd
        def _(pool):
            nc.gpsimd.memset(b1s[:, :], 0.0)
            nc.gpsimd.memset(b2s[:, :], 0.0).then_inc(padded, 1)
            nc.gpsimd.memset(mhalf[:, :], -0.5)
            nc.gpsimd.memset(e_base[:, :], NATURAL)
            nc.gpsimd.memset(ident[:, :], 0.0)
            nc.gpsimd.memset(ident16[:, :], 0.0)
            nc.gpsimd.memset(future16[:, :], 0.0)
            nc.gpsimd.memset(pick[:, :, :], 0.0)
            nc.gpsimd.memset(first_row[:, :], 0.0)
            nc.gpsimd.memset(not_first[:, :], 1.0).then_inc(blank, 1)
            pool.wait_ge(blank, 1)
            for m in (ident, ident16):
                nc.gpsimd.affine_select(out=m[:, :], in_=m[:, :], compare_op=ALU.not_equal, fill=1.0,
                                        base=0, pattern=[[-1, P]], channel_multiplier=1)
            nc.gpsimd.affine_select(out=future16[:, :], in_=future16[:, :], compare_op=ALU.is_gt, fill=-4.0,
                                    base=0, pattern=[[-1, P]], channel_multiplier=1)
            nc.gpsimd.affine_select(out=pick[:, 0, 0:M], in_=pick[:, 0, 0:M], compare_op=ALU.not_equal, fill=1.0,
                                    base=1 - E, pattern=[[0, M]], channel_multiplier=1)
            own = pick[:, 0, M:P].rearrange("e (r c) -> e r c", c=PAD)
            nc.gpsimd.affine_select(out=own, in_=own, compare_op=ALU.not_equal, fill=1.0,
                                    base=0, pattern=[[0, 2], [-1, PAD]], channel_multiplier=1)
            pairs = pick[:, 1:NH, :].rearrange("e q (a m) -> e q a m", a=2)
            nc.gpsimd.affine_select(out=pairs, in_=pairs, compare_op=ALU.not_equal, fill=1.0,
                                    base=0, pattern=[[-2, NJ], [-1, 2], [0, M]], channel_multiplier=1)
            nc.gpsimd.affine_select(out=first_row[:, :], in_=first_row[:, :], compare_op=ALU.not_equal, fill=1.0,
                                    base=0, pattern=[[0, 1]], channel_multiplier=1)
            nc.gpsimd.affine_select(out=not_first[:, :], in_=not_first[:, :], compare_op=ALU.not_equal, fill=0.0,
                                    base=0, pattern=[[0, 1]], channel_multiplier=1)
            nc.gpsimd.iota(prio[:, :, :], pattern=[[0, GT], [-1, E]], base=E, channel_multiplier=0,
                           allow_small_or_imprecise_dtypes=True)
            nc.gpsimd.memset(xnT[:, :, 0:1], 0.0)
            nc.gpsimd.memset(xnT[:, :, T + 1:T + 2], 0.0)
            nc.gpsimd.memset(ohp[:, :, :], 0.0)
            nc.gpsimd.memset(smax[:, :, :], -8.0).then_inc(consts, 1)

            def invert(n):
                pool.wait_ge(var_ready, n + 1)
                nc.gpsimd.tensor_tensor(rstd[:, n], var_e[:, :], mhalf[:, :], ALU.pow).then_inc(rstd_ready, 1)

            def ema_norm():
                pool.wait_ge(knobs_in, 1)
                nc.gpsimd.tensor_tensor(knobs_e[:, :], e_base[:, 0:3], knobs[:, :], ALU.pow).then_inc(knobs_exp, 1)
                pool.wait_ge(ema_ss, 1)
                nc.gpsimd.tensor_tensor(ema_n[:, 1:2], ema_n[:, 0:1], mhalf[:, 0:1], ALU.pow).then_inc(ema_rn, 1)

            def tap_max():
                pool.wait_ge(tap_amax, 1)
                nc.gpsimd.partition_all_reduce(gmax[:, 0:1], amax[:, 0:1], P, RMAX).then_inc(tap_gmax, 1)

            def w_max():
                pool.wait_ge(amax_ready, 1)
                nc.gpsimd.partition_all_reduce(gmax[:, 1:6], amax[:, 1:6], P, RMAX).then_inc(gmax_ready, 1)

            def invert_ss(n):
                pool.wait_ge(ss_bounded, n + 1)
                nc.gpsimd.tensor_tensor(rnorm[:, n % 2], ss_b[:, :], mhalf[:, :], ALU.pow).then_inc(rn_ready, 1)

            def mix_lo(n, c):
                h, k = divmod(c, KD)
                cols = slice(h * GW, (h + 1) * GW)
                pool.wait_ge(xh_done, CHUNKS * n + c + 1)
                nc.gpsimd.tensor_tensor(xmT[:, n % 2, KD + k, cols], mixt[:, c], xmT[:, n % 2, k, cols],
                                        ALU.subtract).then_inc(xl_done, 1)

            def exponent(b):
                pool.wait_ge(expo_ready, b + 1)
                need(pool, gate_ready, b)
                nc.gpsimd.tensor_tensor(novelty[:, :], e_base[:, :], expo[:, :], ALU.pow).then_inc(nov_ready, 1)

            def low(G, q):
                g, m = G % NG, NH * G + q
                pool.wait_ge(hi_done, m + 1)
                nc.gpsimd.tensor_tensor(hl[:, g, q - 1], hm[:, m % 4], hh[:, g, q - 1],
                                        ALU.subtract).then_inc(lo_done, 1)

            def z_invert(G):
                g = G % NG
                pool.wait_ge(zve_ready, G + 1)
                nc.gpsimd.tensor_tensor(zr[:, g], zve[:, g], mhalf[:, 0:GT], ALU.pow).then_inc(zr_ready, 1)

            def times_gamma(G, i):
                g, Y = G % NG, GT * G + i
                pool.wait_ge(w_norm, Y + 1)
                nc.gpsimd.tensor_tensor(z[:, g, i], z[:, g, i], gam[:, :], ALU.mult).then_inc(w_gamma, 1)

            def plus_beta(G, i):
                g, Y = G % NG, GT * G + i
                pool.wait_ge(w_gamma, Y + 1)
                nc.gpsimd.tensor_tensor(z[:, g, i], z[:, g, i], bet[:, :], ALU.add).then_inc(w_affine, 1)

            run({"invert": invert, "ema_norm": ema_norm, "tap_max": tap_max, "w_max": w_max, "invert_ss": invert_ss,
                 "mix_lo": mix_lo, "exponent": exponent, "low": low, "z_invert": z_invert,
                 "times_gamma": times_gamma, "plus_beta": plus_beta})

        @block.scalar
        def _(act):
            def w1_high():
                act.wait_ge(scales_ready, 1)
                nc.scalar.activation(w1h[:, :, EM:EM + M], w1s[:, :, EM:EM + M], ACT.Copy, scale=sc[:, 7:8])
                nc.scalar.activation(w1h[:, :, 0:EM], w1s[:, :, 0:EM], ACT.Copy, scale=sc[:, 3:4]).then_inc(w1_split, 1)

            def w2_high():
                act.wait_ge(scales_ready, 1)
                nc.scalar.activation(w2h[:, :, :], w2s[:, :, :], ACT.Copy, scale=sc[:, 10:11])
                nc.scalar.activation(b2h[:, :], b2s[:, :], ACT.Copy, scale=sc[:, 12:13]).then_inc(w2_split, 1)

            def gelu(n, t):
                X = NT * n + t
                act.wait_ge(xn_ready, X + 1)
                nc.scalar.activation(out_sb[:, n, t], xn_st[:, t % 4], ACT.Gelu_apprx_tanh).then_inc(gelu_done, 1)

            def square(n, t):
                S = NT * n + t
                act.wait_ge(gelu_done, S + 1)
                need(act, ss_ready, S - 1)
                if t == 0:
                    need(act, ss_bounded, n)
                nc.scalar.activation(junk[:, t % 2], out_sb[:, n, t], ACT.Square,
                                     accum_out=ss[:, t:t + 1]).then_inc(ss_ready, 1)

            def keep_x(n, t):
                act.wait_ge(tx_done, NT * n + t + 1)
                if n and (t == 0 or t == GT - 1):
                    act.wait_ge(m2_done, CHUNKS * (n - 1) + KD * ((t + 1) // GT + 1))
                nc.scalar.copy(xnT[:, :, 1 + t * P:1 + (t + 1) * P],
                               rows_in(short("transpose", n, t))).then_inc(xe_done, 1)

            def unit_hi(n, t):
                X = NT * n + t
                if t == 0:
                    act.wait_ge(rn_ready, n + 1)
                need(act, tu_done, X - 3)
                nc.scalar.activation(uh_st[:, t % 4], out_sb[:, n, t], ACT.Copy,
                                     scale=rnorm[:, n % 2, t:t + 1]).then_inc(uh_ready, 1)

            def keep_u(n, t):
                act.wait_ge(tu_done, NT * n + t + 1)
                if t == 0:
                    need(act, sim_ready, NP * (n - 1))
                    need(act, ema_ready, n - 1)
                nc.scalar.copy(uT[:, n % 2, :, t * P:(t + 1) * P],
                               units_in(short("unit_turn", n, t))).then_inc(ue_done, 1)

            def tap0(n, c):
                h, k = divmod(c, KD)
                if k == 0:
                    act.wait_ge(xe_done, NT * n + min(NT, GT * (h + 1) + 1))
                if c == 0:
                    act.wait_ge(taps_ready, 1)
                need(act, xl_done, CHUNKS * (n - 1) + c + 1)
                nc.scalar.activation(mixt[:, c], xnT[:, k, h * GW:(h + 1) * GW], ACT.Copy,
                                     scale=kmix_s[:, 0, k:k + 1]).then_inc(m0_done, 1)

            def mix_hi(n, c):
                h, k = divmod(c, KD)
                act.wait_ge(m2_done, CHUNKS * n + c + 1)
                if c == 0 and n >= 2:
                    act.wait_ge(h_ready, HIDDEN.index(("hidden", NG * (n - 1) - 1, NJ)) + 1)
                nc.scalar.copy(xmT[:, n % 2, k, h * GW:(h + 1) * GW], mixt[:, c]).then_inc(xh_done, 1)

            def tanh(G):
                H = HIDDEN.index(("router", G))
                act.wait_ge(h_ready, H + 1)
                need(act, sco_ready, G)
                nc.scalar.activation(sT[M:2 * M, :], hP[H % 2][M:2 * M, :], ACT.Tanh,
                                     bias=bo1s[M:2 * M, :], scale=sc[M:2 * M, 8:9]).then_inc(tanh_done, 1)

            def keep_h8(G):
                H = HIDDEN.index(("router", G))
                act.wait_ge(h_ready, H + 1)
                need(act, hm_done, NH * (G - 1) + 1)
                nc.scalar.copy(h8[:, :], hP[H % 2][0:M, :]).then_inc(h8_done, 1)

            def keep_pick(G):
                act.wait_ge(ohTP_ready, G + 1)
                need(act, maskP_ready, NH * (G - 1))
                nc.scalar.copy(ohT[:, G % 2], short("pick", G)[0:PAD, :]).then_inc(ohT_ready, 1)

            def keep_mask(G, q):
                m = NH * G + q
                maskP = short("mask", G, q)
                act.wait_ge(maskP_ready, m + 1)
                need(act, hm_done, m - 3)
                if q == 0:
                    need(act, y_ready, GT * (G - 1))
                    nc.scalar.copy(mask_sb[0:M, m % 4], maskP[0:M, :])
                    nc.scalar.copy(tB[M:2 * M, G % NG], maskP[M:2 * M, :]).then_inc(mask_ready, 1)
                else:
                    nc.scalar.copy(mask_sb[:, m % 4], maskP[:, :]).then_inc(mask_ready, 1)

            def high(G, q):
                g = G % NG
                m = NH * G + q
                act.wait_ge(hm_done, m + 1)
                if q == 0:
                    nc.scalar.copy(tB[0:M, g], hm[0:M, m % 4])
                    nc.scalar.copy(tA[0:M, g], hm[0:M, m % 4]).then_inc(hi_done, 1)
                else:
                    nc.scalar.copy(hh[:, g, q - 1], hm[:, m % 4]).then_inc(hi_done, 1)

            def affine(G, i):
                g = G % NG
                act.wait_ge(zb_ready, G + 1)
                nc.scalar.activation(z[:, g, i], z[:, g, i], ACT.Identity, bias=zb[:, g, i:i + 1],
                                     scale=zr[:, g, i:i + 1]).then_inc(w_norm, 1)

            run({"w1_high": w1_high, "w2_high": w2_high, "gelu": gelu, "square": square, "keep_x": keep_x, "tap0": tap0,
                 "mix_hi": mix_hi, "unit_hi": unit_hi, "keep_u": keep_u, "tanh": tanh, "keep_h8": keep_h8,
                 "keep_pick": keep_pick, "keep_mask": keep_mask, "high": high, "affine": affine})

        @block.vector
        def _(dve):
            ts = nc.vector.tensor_scalar
            stt = nc.vector.scalar_tensor_tensor
            tt = nc.vector.tensor_tensor
            count = [0]

            def mark(ins):
                count[0] += 1
                ins.then_inc(own_setup, 1)

            def link(ins):
                mark(ins)
                dve.wait_ge(own_setup, count[0])

            def col(i):
                return sc[:, i:i + 1]

            def ema_norm():
                dve.wait_ge(small_loaded, 16 * len(small_loads))
                ts(knobs[:, 1:3], knobs[:, 1:3], -1.0, None, ALU.mult).then_inc(knobs_in, 1)
                link(tt(ema_sq[:, :], ema_row[:, :], ema_row[:, :], ALU.mult))
                link(nc.vector.reduce_sum(ema_n[:, 0:1], ema_sq[:, :], AX.X))
                ts(ema_n[:, 0:1], ema_n[:, 0:1], NORM_MIN * NORM_MIN, None, ALU.max).then_inc(ema_ss, 1)

            def tap_max():
                dve.wait_ge(small_loaded, 16 * len(small_loads))
                link(nc.vector.tensor_reduce(kabs[:, :], kmix[:, :, :].rearrange("p j k -> p k j"), AX.X, ALU.add,
                                             apply_absolute_value=True))
                nc.vector.reduce_max(amax[:, 0:1], kabs[:, :], AX.X).then_inc(tap_amax, 1)

            def tap_scale():
                dve.wait_ge(tap_gmax, 1)
                link(ts(col(0), gmax[:, 0:1], SCALE_MIN, None, ALU.max))
                link(nc.vector.reciprocal(col(1), col(0)))
                ts(kmix_s[:, :, :], kmix[:, :, :], col(1), None, ALU.mult).then_inc(taps_ready, 1)

            def constants():
                dve.wait_ge(knobs_exp, 1)
                link(ts(tau[:, 3:5], knobs_e[:, 1:3], 1.0, None, ALU.add))
                link(nc.vector.reciprocal(tau[:, 5:7], tau[:, 3:5]))
                nc.vector.tensor_copy(tau[:, 1:2], tau[:, 5:6])
                ts(tau[:, 2:3], tau[:, 5:6], -1.0, 1.0, ALU.mult, ALU.add)
                link(ts(tau[:, 7:8], knobs_e[:, 0:1], -1.0, None, ALU.mult))
                link(tt(tau[:, 3:4], tau[:, 6:7], tau[:, 7:8], ALU.mult))
                link(tt(tau[:, 4:5], tau[:, 7:8], tau[:, 3:4], ALU.subtract))
                dve.wait_ge(ema_rn, 1)
                link(ts(ema_col[:, :], ema_col[:, :], ema_n[:, 1:2], None, ALU.mult))
                link(nc.vector.tensor_copy(ema_hl[:, :, 0], ema_col[:, :]))
                tt(ema_hl[:, :, 1], ema_col[:, :], ema_hl[:, :, 0], ALU.subtract).then_inc(ema_split, 1)

            def w_max():
                dve.wait_ge(w1_loaded, 16 * len(w1_loads))
                nc.vector.tensor_reduce(amax[:, 1:2], w1s[:, :, 0:EM], AX.XY, ALU.max, apply_absolute_value=True)
                nc.vector.tensor_reduce(amax[:, 2:3], w1s[:, :, EM:EM + M], AX.XY, ALU.max, apply_absolute_value=True)
                dve.wait_ge(w2_loaded, 16 * len(w2_loads))
                nc.vector.tensor_reduce(amax[:, 3:4], w2s[:, :, :], AX.XY, ALU.max, apply_absolute_value=True)
                nc.vector.tensor_reduce(amax[:, 4:5], b1s[:, :], AX.X, ALU.max, apply_absolute_value=True)
                nc.vector.tensor_reduce(amax[:, 5:6], b2s[:, :], AX.X, ALU.max,
                                        apply_absolute_value=True).then_inc(amax_ready, 1)

            def w_scale():
                dve.wait_ge(gmax_ready, 1)
                ts(col(6), gmax[:, 2:3], SCALE_MIN, None, ALU.max)
                link(ts(col(2), gmax[:, 4:5], col(1), SCALE_MIN, ALU.mult, ALU.max))
                link(tt(col(2), col(2), gmax[:, 1:2], ALU.max))
                nc.vector.reciprocal(col(7), col(6))
                tt(col(8), col(6), col(0), ALU.mult)
                nc.vector.reciprocal(col(3), col(2))
                link(tt(col(4), col(2), col(0), ALU.mult))
                link(nc.vector.reciprocal(col(5), col(4)))
                link(ts(col(9), gmax[:, 5:6], col(5), SCALE_MIN, ALU.mult, ALU.max))
                link(tt(col(9), col(9), gmax[:, 3:4], ALU.max))
                nc.vector.reciprocal(col(10), col(9))
                link(tt(col(11), col(4), col(9), ALU.mult))
                link(nc.vector.reciprocal(col(12), col(11)))
                link(tt(col(13), col(12), col(12), ALU.mult))
                ts(b1n[:, :], b1s[:, :], col(5), None, ALU.mult)
                ts(col(13), col(13), LN_EPS, None, ALU.mult).then_inc(scales_ready, 1)

            def w1_low():
                dve.wait_ge(w1_split, 1)
                stt(w1l[:, :, 0:EM], w1s[:, :, 0:EM], col(3), w1h[:, :, 0:EM], ALU.mult, ALU.subtract)
                stt(w1l[:, :, EM:EM + M], w1s[:, :, EM:EM + M], col(7), w1h[:, :, EM:EM + M], ALU.mult,
                    ALU.subtract).then_inc(w1_ready, 1)

            def w2_low():
                dve.wait_ge(w2_split, 1)
                stt(w2l[:, :, :], w2s[:, 0:NJ, :], col(10), w2h[:, 0:NJ, :], ALU.mult, ALU.subtract)
                stt(tailB[0:M, :], w2s[0:M, NJ, :], sc[0:M, 10:11], w2h[0:M, NJ, :], ALU.mult, ALU.subtract)
                nc.vector.tensor_copy(tailB[M:M + PAD, :], b2h[M:M + PAD, :])
                stt(tailB[M + PAD:P, :], b2s[M + PAD:P, :], sc[M + PAD:P, 12:13], b2h[M + PAD:P, :], ALU.mult,
                    ALU.subtract).then_inc(w2_ready, 1)

            def row_stats(n, t):
                if n:
                    if t == 0:
                        dve.wait_ge(x_loaded[n - 1], 16)
                elif t % GT == 0:
                    dve.wait_ge(x0_loaded[t // GT], 16)
                nc.vector.bn_stats(stats[:, t], x_sb[:, n, t]).then_inc(st_ready, 1)

            def variance(n):
                dve.wait_ge(st_ready, NT * (n + 1))
                for t in range(NT):
                    last = nc.vector.bn_aggr(mv[:, t], stats[:, t])
                last.then_inc(mv_ready, 1)
                dve.wait_ge(mv_ready, n + 1)
                need(dve, rstd_ready, n)
                ts(var_e[:, :], mv[:, :, 1], LN_EPS, None, ALU.add).then_inc(var_ready, 1)

            def shift(n):
                dve.wait_ge(rstd_ready, n + 1)
                stt(nbias[:, n % 2], mv[:, :, 0], -1.0, rstd[:, n], ALU.mult, ALU.mult).then_inc(nb_ready, 1)

            def norm(n, t):
                X = NT * n + t
                dve.wait_ge(nb_ready, n + 1)
                need(dve, tx_done, X - 3)
                need(dve, gelu_done, X - 3)
                ts(xn_st[:, t % 4], x_sb[:, n, t], rstd[:, n, t:t + 1], nbias[:, n % 2, t:t + 1],
                   ALU.mult, ALU.add).then_inc(xn_ready, 1)

            def bound_ss(n):
                dve.wait_ge(ss_ready, NT * n + NT)
                ts(ss_b[:, :], ss[:, :], NORM_MIN * NORM_MIN, None, ALU.max).then_inc(ss_bounded, 1)

            def unit_lo(n, t):
                dve.wait_ge(uh_ready, NT * n + t + 1)
                stt(ul_st[:, t % 4], out_sb[:, n, t], rnorm[:, n % 2, t:t + 1], uh_st[:, t % 4],
                    ALU.mult, ALU.subtract).then_inc(ul_ready, 1)

            def tap1(n, c):
                h, k = divmod(c, KD)
                dve.wait_ge(m0_done, CHUNKS * n + c + 1)
                stt(mixt[:, c], xnT[:, k, 1 + h * GW:1 + (h + 1) * GW], kmix_s[:, 1, k:k + 1], mixt[:, c],
                    ALU.mult, ALU.add).then_inc(m1_done, 1)

            def tap2(n, c):
                h, k = divmod(c, KD)
                dve.wait_ge(m1_done, CHUNKS * n + c + 1)
                stt(mixt[:, c], xnT[:, k, 2 + h * GW:2 + (h + 1) * GW], kmix_s[:, 2, k:k + 1], mixt[:, c],
                    ALU.mult, ALU.add).then_inc(m2_done, 1)

            def inv_(b):
                ts(inv[:, b], rstd[:, b], sc[:, 12:13], None, ALU.mult).then_inc(inv_ready, 1)

            def ema_sum(b):
                dve.wait_ge(ema_ready, b + 1)
                need(dve, expo_ready, b)
                nc.vector.reduce_sum(ems[:, :], ema_in(short("ema_dot", b)), AX.X).then_inc(ems_ready, 1)

            def sim_max(b, q):
                t, lo, hi = PIECES[q]
                if q == 0:
                    need(dve, expo_ready, b)
                dve.wait_ge(sim_ready, NP * b + q + 1)
                nc.vector.reduce_max(smax[:, t, lo // 4:lo // 4 + 1], simP[q % 2][:, 0:(hi - lo) * P],
                                     AX.X).then_inc(sim_free, 1)

            def familiar(b):
                n = [0]

                def chain(ins):
                    n[0] += 1
                    ins.then_inc(own_gate, 1)
                    dve.wait_ge(own_gate, 4 * b + n[0])

                dve.wait_ge(sim_free, NP * b + NP)
                dve.wait_ge(ems_ready, b + 1)
                need(dve, nov_ready, b)
                chain(tt(seq[:, :], smax[:, :, 0], smax[:, :, 1], ALU.max))
                chain(ts(fix[:, :], ems[:, 0:1], first_row[:, :], None, ALU.mult))
                chain(stt(seq[:, 0:1], seq[:, 0:1], not_first[:, :], fix[:, :], ALU.mult, ALU.add))
                chain(ts(seq[:, :], seq[:, :], tau[:, 3:4], None, ALU.mult))
                stt(expo[:, :], ems[:, :], tau[:, 4:5], seq[:, :], ALU.mult, ALU.add).then_inc(expo_ready, 1)

            def gate_(b):
                dve.wait_ge(nov_ready, b + 1)
                ts(gate[:, b], novelty[:, :], tau[:, 1:2], tau[:, 2:3], ALU.mult, ALU.add).then_inc(gate_ready, 1)

            def argmax(G):
                n = [0]

                def chain(ins):
                    n[0] += 1
                    ins.then_inc(own_argmax, 1)
                    dve.wait_ge(own_argmax, 5 * G + n[0])

                def over(v):
                    return v.to_broadcast([P, GT, E])

                dve.wait_ge(sco_ready, G + 1)
                need(dve, ohTP_ready, G)
                chain(tt(sco[:, :, :], scores_in(short("scores", G)),
                         bo2r[:, :].unsqueeze(1).to_broadcast([P, GT, E]), ALU.add))
                chain(nc.vector.reduce_max(top[:, :, 0], sco[:, :, :], AX.X))
                chain(tt(sco[:, :, :], sco[:, :, :], over(top[:, :, 0:1]), ALU.is_ge))
                chain(tt(sco[:, :, :], sco[:, :, :], prio[:, :, :], ALU.mult))
                chain(nc.vector.reduce_max(top[:, :, 1], sco[:, :, :], AX.X))
                tt(ohp[:, :, 0:E], sco[:, :, :], over(top[:, :, 1:2]), ALU.is_equal).then_inc(oh_ready, 1)

            def masked(G, q):
                m = NH * G + q
                dve.wait_ge(mask_ready, m + 1)
                if m >= 4:
                    G2, q2 = divmod(m - 4, NH)
                    if q2:
                        dve.wait_ge(lo_done, NJ * G2 + q2)
                    else:
                        dve.wait_ge(lo8_done, G2 + 1)
                if q == 0:
                    dve.wait_ge(h8_done, G + 1)
                    stt(hm[0:M, m % 4], h8[:, :], b1n[0:M, NJ:NJ + 1], mask_sb[0:M, m % 4],
                        ALU.add, ALU.mult).then_inc(hm_done, 1)
                else:
                    H = HIDDEN.index(("hidden", G, q))
                    dve.wait_ge(h_ready, H + 1)
                    stt(hm[:, m % 4], hP[H % 2][:, :], b1n[:, q - 1:q], mask_sb[:, m % 4],
                        ALU.add, ALU.mult).then_inc(hm_done, 1)

            def low8(G):
                m = NH * G
                dve.wait_ge(hi_done, m + 1)
                tt(tA[M:2 * M, G % NG], hm[0:M, m % 4], tA[0:M, G % NG], ALU.subtract).then_inc(lo8_done, 1)

            def residual(G, i):
                b, g = divmod(G, NG)
                Y = GT * G + i
                dve.wait_ge(y_ready, Y + 1)
                need(dve, result_ready, Y + 1 - NG * GT)
                if i == 0:
                    dve.wait_ge(inv_ready, b + 1)
                stt(z[:, g, i], x_sb[:, b, g * GT + i], inv[:, b, g * GT + i:g * GT + i + 1], yP[:, :], ALU.mult,
                    ALU.add).then_inc(z_done, 1)

            def z_stats(G, i):
                dve.wait_ge(z_done, GT * G + i + 1)
                nc.vector.bn_stats(zst[:, i], z[:, G % NG, i]).then_inc(zst_ready, 1)

            def z_var(G):
                g = G % NG
                dve.wait_ge(zst_ready, GT * G + GT)
                for i in range(GT):
                    last = nc.vector.bn_aggr(zmv[:, g, i], zst[:, i])
                last.then_inc(zmv_ready, 1)
                dve.wait_ge(zmv_ready, G + 1)
                ts(zve[:, g], zmv[:, g, :, 1], sc[:, 13:14], None, ALU.add).then_inc(zve_ready, 1)

            def z_shift(G):
                g = G % NG
                dve.wait_ge(zr_ready, G + 1)
                stt(zb[:, g], zmv[:, g, :, 0], -1.0, zr[:, g], ALU.mult, ALU.mult).then_inc(zb_ready, 1)

            def gated_(G, i):
                b, g = divmod(G, NG)
                t = g * GT + i
                dve.wait_ge(gate_ready, b + 1)
                stt(out_sb[:, b, t], out_sb[:, b, t], gate[:, b, t:t + 1], x_sb[:, b, t],
                    ALU.mult, ALU.add).then_inc(gated, 1)

            def final(G, i):
                b, g = divmod(G, NG)
                t = g * GT + i
                Y = GT * G + i
                dve.wait_ge(w_affine, Y + 1)
                dve.wait_ge(gated, Y + 1)
                tt(out_sb[:, b, t], out_sb[:, b, t], z[:, g, i], ALU.add).then_inc(result_ready, 1)

            run({"ema_norm": ema_norm, "tap_max": tap_max, "tap_scale": tap_scale, "constants": constants,
                 "w_max": w_max, "w_scale": w_scale, "w1_low": w1_low, "w2_low": w2_low, "row_stats": row_stats, "variance": variance, "shift": shift,
                 "norm": norm, "bound_ss": bound_ss, "unit_lo": unit_lo, "tap1": tap1, "tap2": tap2, "inv": inv_,
                 "ema_sum": ema_sum, "sim_max": sim_max, "familiar": familiar, "gate": gate_, "argmax": argmax,
                 "masked": masked, "low8": low8, "residual": residual, "z_stats": z_stats, "z_var": z_var,
                 "z_shift": z_shift, "gated": gated_, "final": final})

        @block.tensor
        def _(pe):
            mm = nc.tensor.matmul

            def short_free(*use):
                S = SHORT.index(use)
                if S < 3:
                    return
                name, *args = SHORT[S - 3]
                n = args[0]
                if name == "transpose":
                    pe.wait_ge(xe_done, NT * n + args[1] + 1)
                elif name == "unit_turn":
                    pe.wait_ge(ue_done, NT * n + args[1] + 1)
                elif name == "scores":
                    pe.wait_ge(own_argmax, 5 * n + 1)
                elif name == "ema_dot":
                    pe.wait_ge(ems_ready, n + 1)
                elif name == "pick":
                    pe.wait_ge(ohT_ready, n + 1)
                else:
                    pe.wait_ge(mask_ready, NH * n + args[1] + 1)

            def transpose(n, t):
                X = NT * n + t
                if X == 0:
                    pe.wait_ge(consts, 1)
                pe.wait_ge(xn_ready, X + 1)
                short_free("transpose", n, t)
                rows = rows_in(short("transpose", n, t))
                for k in range(KD):
                    last = nc.tensor.transpose(rows[:, k], xn_st[:, t % 4, k * P:(k + 1) * P], ident[:, :])
                last.then_inc(tx_done, 1)

            def unit_turn(n, t):
                X = NT * n + t
                pe.wait_ge(ul_ready, X + 1)
                short_free("unit_turn", n, t)
                units = units_in(short("unit_turn", n, t))
                for part, st in enumerate((uh_st, ul_st)):
                    for k in range(KD):
                        last = nc.tensor.transpose(units[:, part * KD + k], st[:, t % 4, k * P:(k + 1) * P],
                                                   ident16[:, :])
                last.then_inc(tu_done, 1)

            def ema_dot(b):
                u = uT[:, b % 2]
                pe.wait_ge(ue_done, NT * b + NT)
                pe.wait_ge(ema_split, 1)
                short_free("ema_dot", b)
                sums = ema_in(short("ema_dot", b))
                for t in range(NT):
                    for n, (i, k) in enumerate((i, k) for i in range(2) for k in range(KD)):
                        last = mm(sums[:, t], u[:, i * KD + k, t * P:(t + 1) * P], ema_hl[:, k, :],
                                  start=(n == 0), stop=(n == 2 * KD - 1))
                last.then_inc(ema_ready, 1)

            def sim(b, q):
                t, lo, hi = PIECES[q]
                u = uT[:, b % 2]
                pe.wait_ge(ue_done, NT * b + t + 1)
                need(pe, sim_free, NP * b + q - 1)
                w = (hi - lo) * P
                bank = simP[q % 2]
                terms = [(i, j, k) for i, j in PAIRS for k in range(KD)]
                for n, (i, j, k) in enumerate(terms):
                    last = mm(bank[:, 0:w], u[:, i * KD + k, t * P:(t + 1) * P],
                              u[:, j * KD + k, lo * P:hi * P], start=(n == 0), stop=(n == len(terms) - 1))
                    if n == 0 and hi == t + 1:
                        mm(bank[:, w - P:w], ident16[:, :], future16[:, :], start=False, stop=False)
                last.then_inc(sim_ready, 1)

            def hidden(G, q):
                b, g = divmod(G, NG)
                H = HIDDEN.index(("hidden", G, q) if q else ("router", G))
                if H >= 2:
                    name, *old = HIDDEN[H - 2]
                    if name == "hidden":
                        pe.wait_ge(hm_done, NH * old[0] + old[1] + 1)
                    else:
                        pe.wait_ge(h8_done, old[0] + 1)
                        pe.wait_ge(tanh_done, old[0] + 1)
                cols = slice(NJ * 2 * M, NJ * 2 * M + P) if q == 0 else slice((q - 1) * P, q * P)
                terms = [(i, j, k) for i, j in PAIRS for k in range(KD)]
                for n, (i, j, k) in enumerate(terms):
                    last = mm(hP[H % 2][:, :], (w1h, w1l)[i][:, k, cols],
                              xmT[:, b % 2, j * KD + k, g * GW:(g + 1) * GW], start=(n == 0),
                              stop=(n == len(terms) - 1))
                last.then_inc(h_ready, 1)

            def router(G):
                b, g = divmod(G, NG)
                pe.wait_ge(w1_ready, 1)
                pe.wait_ge(xl_done, CHUNKS * b + KD * (g + 1))
                hidden(G, 0)

            def scores(G):
                pe.wait_ge(tanh_done, G + 1)
                short_free("scores", G)
                bank = scores_in(short("scores", G))
                for i in range(GT):
                    last = mm(bank[:, i], sT[M:2 * M, i * P:(i + 1) * P], wo2s[M:2 * M, :], start=True, stop=True)
                last.then_inc(sco_ready, 1)

            def pick_(G):
                pe.wait_ge(oh_ready, G + 1)
                short_free("pick", G)
                bank = short("pick", G)
                for i in range(GT):
                    last = mm(bank[0:PAD, i * P:(i + 1) * P], ohp[:, i, :], ident16[:, :], start=True, stop=True)
                last.then_inc(ohTP_ready, 1)

            def mask(G, q):
                pe.wait_ge(ohT_ready, G + 1)
                short_free("mask", G, q)
                mm(short("mask", G, q)[:, :], pick[:, q, :], ohT[:, G % 2], start=True,
                   stop=True).then_inc(maskP_ready, 1)

            def expert(G, i):
                g = G % NG
                Y = GT * G + i
                need(pe, z_done, Y)
                if i == 0:
                    pe.wait_ge(lo8_done, G + 1)
                    pe.wait_ge(lo_done, NJ * (G + 1))
                    pe.wait_ge(w2_ready, 1)
                cols = slice(i * P, (i + 1) * P)
                mm(yP[:, :], tA[:, g, cols], w2h[:, NJ], start=True, stop=False)
                mm(yP[:, :], tB[:, g, cols], tailB[:, :], start=False, stop=False)
                for j in range(NJ):
                    mm(yP[:, :], hh[:, g, j, cols], w2h[:, j], start=False, stop=False)
                    mm(yP[:, :], hl[:, g, j, cols], w2h[:, j], start=False, stop=False)
                    last = mm(yP[:, :], hh[:, g, j, cols], w2l[:, j], start=False, stop=(j == NJ - 1))
                last.then_inc(y_ready, 1)

            run({"transpose": transpose, "unit_turn": unit_turn, "ema_dot": ema_dot, "sim": sim, "hidden": hidden,
                 "router": router, "scores": scores, "pick": pick_, "mask": mask, "expert": expert})


_INS = ["L0_attn_x", "L0_attn_ema_out", "L0_attn_log_tau", "L0_attn_log_blend", "L0_attn_logit_blend_seq",
        "L0_ffn_mix_kernel", "L0_ffn_W1", "L0_ffn_b1", "L0_ffn_W2", "L0_ffn_b2", "L0_ffn_Wo1", "L0_ffn_bo1",
        "L0_ffn_Wo2", "L0_ffn_bo2", "L0_ffn_gamma", "L0_ffn_beta"]


def kernel(**inputs):
    import numpy as _np
    import concourse.bacc as _bacc
    from concourse import mybir as _mybir
    from concourse.bass_utils import run_bass_kernel_spmd as _run

    nc = _bacc.Bacc("TRN2", target_bir_lowering=False, num_devices=1)
    arrays, args = {}, []
    for name in _INS:
        a = _np.ascontiguousarray(inputs[name])
        if a.ndim == 0:
            a = a.reshape(1)
        arrays[f"in_{name}"] = a
        args.append(nc.dram_tensor(f"in_{name}", a.shape, _mybir.dt.from_np(a.dtype), kind="ExternalInput").ap())
    shape = arrays["in_L0_attn_x"].shape
    out = nc.dram_tensor("out_0", shape, _mybir.dt.float32, kind="ExternalOutput").ap()
    build(nc, *args, out)
    r = _run(nc, [arrays], core_ids=[0])
    return r.results[0]["out_0"]
```

```python
from contextlib import ExitStack

import concourse.bass as bass
from concourse import mybir

F32 = mybir.dt.float32
F16 = mybir.dt.float16
ALU = mybir.AluOpType
ACT = mybir.ActivationFunctionType
AX = mybir.AxisListType
RMAX = bass.bass_isa.ReduceOp.max

P = 128
LN_EPS = 1e-5
NORM_MIN = 1e-12
SCALE_MIN = 1e-4
NATURAL = 2.718281828459045


PLAN = dict(
    row_stats=(-14.45, 0.2), variance=(-13.3, 0.35), invert=(-15.91, 0.7), shift=(-10.61, 0.6),
    norm=(-9.6, 0.4), transpose=(-8.15, 0.45), gelu=(-8.75, 0.4), square=(-8.75, 0.45), keep_x=(-7.85, 0.5),
    bound_ss=(-5, 0.31), invert_ss=(-5.69, 0.6), tap0=(-5.73, 0.75), tap1=(-5.55, 0.95), tap2=(-4.94, 0.8),
    mix_hi=(-3.6, 0.7), mix_lo=(-3.65, 0.5), unit=(-2.96, 0.2), unit_turn=(-2.9, 0.3), unit_hi=(-2.66, 0.35),
    unit_lo=(-2.75, 0.3),
    inv=(-0.89, 0), ema_dot=(3.4, 0), ema_sum=(4.55, 0), sim=(0.2, 0.65), sim_max=(0.75, 0.65),
    familiar=(8.54, 0), exponent=(7.5, 0), gate=(9, 0),
    router=(-2.55, 0), tanh=(-2.04, 0), keep_h8=(-0.87, 0), scores=(-2.05, 0), argmax=(-1.89, 0.005),
    pick=(-1.74, 0), keep_pick=(-1.4, 0), hidden=(-0.84, 0.75), masked=(-0.45, 0.7), high=(-0.11, 0.75),
    low=(-0.2, 0.6), low8=(1, 0), expert=(3.5, 0.7), residual=(3.5, 0.85), z_stats=(3.7, 1.05), z_var=(7.5, 0),
    z_invert=(7.3, 0), z_shift=(8.59, 0), affine=(8.7, 0.6), times_gamma=(8.75, 0.55), plus_beta=(9.45, 0.35),
    gated=(9.6, 0.05), final=(10.25, 0.2), share=(-3.91, 0), fetch=(-1.81, 0), fetch_tail=(-0.59, 0),
    ema_norm=(-14.94, 0), tap_max=(-22.75, 0), tap_scale=(-19.25, 0), constants=(-14.8, 0), w_max=(-11.3, 0),
    w_scale=(-8.11, 0), w1_high=(-7.55, 0), w1_low=(-6.55, 0), w2_high=(-1.35, 0), w2_low=(-3.99, 0),
)
FIRST = dict(
    PLAN,
    row_stats=(-23.75, 0.1), variance=(-22.83, 0.05), invert=(-25.62, 0.1), shift=(-22, 0.6),
    norm=(-21.5, 0.55), transpose=(-19.36, 0.15), gelu=(-19.4, 0.7), square=(-17.15, 0.6), keep_x=(-19.1, 0.65),
    bound_ss=(-11.15, 0.45), invert_ss=(-11.21, 0.7), tap0=(-12.05, 0.7), tap1=(-8.9, 0.5), tap2=(-7.71, 0.9),
    mix_hi=(-7.6, 0.6), mix_lo=(-9.53, 0.45), unit=(-9.19, 0.35), unit_turn=(-16.35, 1.3),
    unit_hi=(-8.21, 0.25), unit_lo=(-7.25, 0.25),
    inv=(-2.29, 0), ema_dot=(0.07, 0), ema_sum=(-0.35, 0), sim=(-2.35, 0.55), sim_max=(-2.65, 0.6),
    familiar=(6.68, 0), exponent=(7.6, 0), gate=(8.75, 0),
    router=(-7.1, 0), tanh=(-5.94, 0), keep_h8=(-5.05, 0), scores=(-2.95, 0), argmax=(-4.85, 0.25),
    pick=(-1.71, 0), keep_pick=(-5.19, 0), hidden=(-0.49, 0.5), masked=(-0.35, 0.6), high=(0.54, 0.55),
    low=(-5.93, 1.3), expert=(3.15, 0.8), residual=(3.25, 1.05), z_stats=(3.51, 1.05), z_var=(7.2, 0),
    z_invert=(7.07, 0), z_shift=(8.13, 0), affine=(8.65, 0.45), times_gamma=(8.19, 0.4), plus_beta=(8.55, 0.8),
    gated=(9.41, 0.1), final=(11, 0.25), share=(-11.37, 0), fetch=(-5.51, 0), fetch_tail=(-1.8, 0),
)
LAST = dict(
    PLAN,
    row_stats=(-15.45, 0.1), variance=(-13.2, 0.4), invert=(-13.16, 0.4), shift=(-10.61, 0.8), norm=(-8.8, 0.3),
    transpose=(-7.95, 0.4), gelu=(-7.9, 0.4), square=(-7.75, 0.45), keep_x=(-7.6, 0.45), bound_ss=(-3.89, 0.35),
    invert_ss=(-4.31, 0.6), tap0=(-5.4, 0.6), tap1=(-5.25, 0.65), tap2=(-4.81, 0.6), mix_hi=(-4.2, 0.65),
    mix_lo=(-5.15, 1.25), unit=(-2.84, 0.35), unit_turn=(-2.32, 0.4), unit_hi=(-1.99, 0.35),
    unit_lo=(-1.85, 0.4),
    inv=(-1.07, 0), ema_dot=(3.2, 0), ema_sum=(3.35, 0), sim=(0.4, 0.65), sim_max=(0.95, 0.6),
    familiar=(7.78, 0), exponent=(8.09, 0), gate=(8.6, 0),
    router=(-3.99, 0), tanh=(-4.06, 0), keep_h8=(-3.05, 0), scores=(-3.55, 0), argmax=(-2.65, 0.05),
    pick=(-2.01, 0), keep_pick=(-1.34, 0), hidden=(-1.4, 0.55), masked=(-0.81, 0.4), high=(-0.66, 0.35),
    low=(-1.3, 0.75), low8=(0.1, 0), expert=(8.04, 0.95), residual=(4, 0.95), z_stats=(4.19, 1.45),
    z_var=(8.8, 0), z_invert=(8.48, 0), z_shift=(12.96, 0), affine=(11.52, 1.3), times_gamma=(18.35, 1.1),
    plus_beta=(19.5, 2), gated=(14.21, 1.35), final=(26.25, 2.7), share=(-4.52, 0), fetch=(-4.28, 0),
    fetch_tail=(-3.9, 0),
)
SETUP = ("ema_norm", "tap_max", "tap_scale", "constants", "w_max", "w_scale", "w1_high", "w1_low", "w2_high",
         "w2_low")
FRONT = ("row_stats", "variance", "invert", "shift", "norm", "transpose", "gelu", "square", "keep_x", "bound_ss",
         "invert_ss", "tap0", "tap1", "tap2", "mix_hi", "mix_lo", "unit_hi", "unit_lo", "unit_turn", "unit")
SIM = ("inv", "ema_dot", "ema_sum", "sim", "sim_max", "familiar", "exponent", "gate")
BATCH_STEPS = dict(
    row_stats="tiles", variance="halves", invert="halves", shift="halves", bound_ss="halves",
    invert_ss="halves", norm="tiles", transpose="tiles", gelu="tiles", square="tiles", keep_x="tiles",
    tap0="chunks", tap1="chunks", tap2="chunks", mix_hi="chunks", mix_lo="chunks", unit_hi="tiles",
    unit_lo="tiles", unit_turn="tiles", unit="tiles", sim="pieces", sim_max="pieces",
)
GROUP_STEPS = dict(
    argmax="decisions", hidden="pairs", masked="blocks", high="blocks", low="pairs", expert="rows",
    residual="rows", z_stats="rows", affine="rows", times_gamma="rows", plus_beta="rows", gated="rows",
    final="rows",
)


def order(names, batches, groups, counts):
    at = []
    for name in names:
        if name in SETUP:
            at.append((PLAN[name][0], name, ()))
        elif name in FRONT or name in SIM:
            for b in range(batches):
                start, step = (FIRST if b == 0 else LAST if b == batches - 1 else PLAN)[name]
                n = counts[BATCH_STEPS[name]] if name in BATCH_STEPS else 0
                at += [(8 * b + start + step * i, name, (b, i)) for i in range(n)] or [(8 * b + start, name, (b,))]
        else:
            for G in range(groups * batches):
                start, step = (LAST if G == groups * batches - 1 else FIRST if G == 0 else PLAN)[name]
                n = counts[GROUP_STEPS[name]] if name in GROUP_STEPS else 0
                first = 1 if name in ("hidden", "low") else 0
                at += [(8 / groups * G + start + step * i, name, (G, i)) for i in range(first, n)] or \
                    [(8 / groups * G + start, name, (G,))]
    at.sort(key=lambda entry: entry[0])
    return [(name, *args) for _, name, args in at]


def build(nc, x, ema, log_tau, log_blend, logit_seq, mix_k, W1, b1, W2, b2, Wo1, bo1, Wo2, bo2,
          gamma, beta, out):
    B, T, D = x.shape
    E, _, M = W1.shape
    NT = T // P
    KD = D // P
    GT = 4
    NG = NT // GT
    GW = GT * P
    NJ = E // 2
    NH = NJ + 1
    EM = E * M
    PAD = 32
    CHUNKS = NG * KD
    PIECES = [(t, 0, min(t + 1, 4)) for t in range(4)]
    PIECES += [p for t in range(4, NT) for p in ((t, 0, 4), (t, 4, t + 1))]
    NP = len(PIECES)
    PAIRS = ((0, 0), (0, 1), (1, 0))

    COUNTS = dict(tiles=NT, chunks=CHUNKS, pieces=NP, rows=GT, blocks=NH, pairs=NH, decisions=6, halves=NG)

    def in_order(names):
        return order(names, B, NG, COUNTS)

    HIDDEN = in_order(("router", "hidden"))
    SHORT = in_order(("transpose", "unit_turn", "scores", "ema_dot", "pick"))

    ctx = ExitStack()
    with ctx:
        def sb(name, shape, dt=F32):
            return ctx.enter_context(nc.sbuf_tensor(name, shape, dt))

        def ps(name, shape, dt=F32):
            return ctx.enter_context(nc.psum_tensor(name, shape, dt))

        def sem(name):
            return ctx.enter_context(nc.semaphore(name))

        ident = sb("ident", [P, P])
        ident16 = sb("ident16", [P, P], F16)
        future16 = sb("future16", [P, P], F16)
        prio = sb("prio", [P, GT, E])
        mhalf = sb("mhalf", [P, NT])
        e_base = sb("e_base", [P, NT])
        first_row = sb("first_row", [P, 1])
        not_first = sb("not_first", [P, 1])
        knobs = sb("knobs", [P, 3])
        knobs_e = sb("knobs_e", [P, 3])
        tau = sb("tau", [P, 8])
        kmix = sb("kmix", [P, 3, KD])
        kmix_s = sb("kmix_s", [P, 3, KD])
        kabs = sb("kabs", [P, KD])
        ema_row = sb("ema_row", [P, D])
        ema_sq = sb("ema_sq", [P, D])
        ema_n = sb("ema_n", [P, 2])
        ema_col = sb("ema_col", [P, KD])
        ema_hl = sb("ema_hl", [P, KD, 2], F16)
        w1s = sb("w1s", [P, KD, EM + M])
        w1h = sb("w1h", [P, KD, EM + M], F16)
        w1l = sb("w1l", [P, KD, EM + M], F16)
        w2s = sb("w2s", [P, NJ + 1, D])
        w2h = sb("w2h", [P, NJ + 1, D], F16)
        w2l = sb("w2l", [P, NJ, D], F16)
        b2s = sb("b2s", [P, D])
        tailB = sb("tailB", [P, D], F16)
        b2h = sb("b2h", [P, D], F16)
        b1s = sb("b1s", [P, NJ + 1])
        b1n = sb("b1n", [P, NJ + 1])
        bo1s = sb("bo1s", [P, 1])
        wo2s = sb("wo2s", [P, E])
        bo2r = sb("bo2r", [P, E])
        gam = sb("gam", [P, D])
        bet = sb("bet", [P, D])
        amax = sb("amax", [P, 6])
        gmax = sb("gmax", [P, 6])
        sc = sb("sc", [P, 24])

        x_sb = sb("x_sb", [P, B, NT, D])
        out_sb = sb("out_sb", [P, B, NT, D])
        rstd = sb("rstd", [P, B, NT])
        gate = sb("gate", [P, B, NT])
        inv = sb("inv", [P, B, NT])

        uT = sb("uT", [P, 2, 2 * KD, T], F16)
        xmT = sb("xmT", [P, 2, 2 * KD, T], F16)

        stats = sb("stats", [P, 2, NT, 6])
        mv = sb("mv", [P, 2, NT, 2])
        var_e = sb("var_e", [P, NT])
        nbias = sb("nbias", [P, 2, NT])
        ss = sb("ss", [P, NT])
        ss_b = sb("ss_b", [P, NT])
        rnorm = sb("rnorm", [P, 2, NT])
        xn_st = sb("xn_st", [P, 4, D])
        junk = sb("junk", [P, 2, D])
        unit_st = sb("unit_st", [P, 4, D])
        xnT = sb("xnT", [P, KD, T + 2])
        mixt = sb("mixt", [P, CHUNKS, GW])

        smax = sb("smax", [P, NT, 2])
        seq = sb("seq", [P, NT])
        ems = sb("ems", [P, NT])
        fix = sb("fix", [P, 1])
        expo = sb("expo", [P, NT])
        novelty = sb("novelty", [P, NT])

        sT = sb("sT", [P, GW])
        h8 = sb("h8", [M, GW])
        sco = sb("sco", [P, GT, E])
        top = sb("top", [P, GT, 2])
        ohp = sb("ohp", [P, GT, PAD], F16)
        ohT = sb("ohT", [PAD, 2, GW], F16)
        mask_sb = sb("mask_sb", [P, NG, NJ, GW], F16)
        mask8 = sb("mask8", [M, NG, GW], F16)
        hm = sb("hm", [P, 4, GW])
        hh = sb("hh", [P, NG, NJ, GW], F16)
        hl = sb("hl", [P, NG, NJ, GW], F16)
        tA = sb("tA", [P, NG, GW], F16)
        tB = sb("tB", [P, NG, GW], F16)
        z = sb("z", [P, NG, GT, D])
        zst = sb("zst", [P, NG, GT, 6])
        zmv = sb("zmv", [P, NG, GT, 2])
        zve = sb("zve", [P, NG, GT])
        zr = sb("zr", [P, NG, GT])
        zb = sb("zb", [P, NG, GT])

        onehots = nc.dram_tensor("onehots", [NG, PAD, GW], F16).ap()

        simP = [ps(f"simP{i}", [P, 512]) for i in range(2)]
        hP = [ps(f"hP{i}", [P, GW]) for i in range(2)]
        yP = ps("yP", [P, D])
        shortP = [ps(f"shortP{i}", [P, 512]) for i in range(3)]

        def short(*use):
            return shortP[SHORT.index(use) % 3]

        def rows_in(bank):
            return bank[:, 0:KD * P].rearrange("p (k q) -> p k q", k=KD)

        def scores_in(bank):
            return bank[:, 0:GT * E].rearrange("p (i e) -> p i e", i=GT)

        def ema_in(bank):
            return bank[:, 0:2 * NT].rearrange("p (t c) -> p t c", c=2)

        padded = sem("padded")
        small_loaded = sem("small_loaded")
        w1_loaded = sem("w1_loaded")
        w2_loaded = sem("w2_loaded")
        result_ready = sem("result_ready")
        pool_result = sem("pool_result")
        stored = sem("stored")
        blank = sem("blank")
        consts = sem("consts")
        var_ready = sem("var_ready")
        rstd_ready = sem("rstd_ready")
        knobs_in = sem("knobs_in")
        knobs_exp = sem("knobs_exp")
        ema_ss = sem("ema_ss")
        ema_rn = sem("ema_rn")
        tap_amax = sem("tap_amax")
        tap_gmax = sem("tap_gmax")
        amax_ready = sem("amax_ready")
        gmax_ready = sem("gmax_ready")
        ss_bounded = sem("ss_bounded")
        rn_ready = sem("rn_ready")
        xh_done = sem("xh_done")
        xl_done = sem("xl_done")
        expo_ready = sem("expo_ready")
        nov_ready = sem("nov_ready")
        hi_done = sem("hi_done")
        lo_done = sem("lo_done")
        zve_ready = sem("zve_ready")
        zr_ready = sem("zr_ready")
        w_norm = sem("w_norm")
        w_gamma = sem("w_gamma")
        w_affine = sem("w_affine")
        scales_ready = sem("scales_ready")
        w1_split = sem("w1_split")
        w2_split = sem("w2_split")
        w2_parts = sem("w2_parts")
        gelu_done = sem("gelu_done")
        ss_ready = sem("ss_ready")
        xn_ready = sem("xn_ready")
        tx_done = sem("tx_done")
        m2_done = sem("m2_done")
        xe_done = sem("xe_done")
        tu_done = sem("tu_done")
        uh_ready = sem("uh_ready")
        h_ready = sem("h_ready")
        sim_ready = sem("sim_ready")
        ue_done = sem("ue_done")
        taps_ready = sem("taps_ready")
        m0_done = sem("m0_done")
        sco_ready = sem("sco_ready")
        tanh_done = sem("tanh_done")
        hm_done = sem("hm_done")
        h8_done = sem("h8_done")
        ohTP_ready = sem("ohTP_ready")
        ohT_ready = sem("ohT_ready")
        shared = sem("shared")
        masks_in = [sem(f"masks_in{g}") for g in range(NG)]
        onehots_in = [sem(f"onehots_in{g}") for g in range(NG)]
        y_ready = sem("y_ready")
        zb_ready = sem("zb_ready")
        last_gamma = sem("last_gamma")
        last_affine = sem("last_affine")
        own_setup = sem("own_setup")
        ema_split = sem("ema_split")
        w1_ready = sem("w1_ready")
        w2_ready = sem("w2_ready")
        st_ready = sem("st_ready")
        mv_ready = sem("mv_ready")
        nb_ready = sem("nb_ready")
        unit_ready = sem("unit_ready")
        m1_done = sem("m1_done")
        inv_ready = sem("inv_ready")
        ema_ready = sem("ema_ready")
        ems_ready = sem("ems_ready")
        sim_free = sem("sim_free")
        own_gate = sem("own_gate")
        gate_ready = sem("gate_ready")
        own_argmax = sem("own_argmax")
        oh_ready = sem("oh_ready")
        lo8_done = sem("lo8_done")
        z_done = sem("z_done")
        zst_ready = sem("zst_ready")
        zmv_ready = sem("zmv_ready")
        gated = sem("gated")
        x0_loaded = [sem(f"x0_loaded{i}") for i in range(NT // 2)]
        x_loaded = [sem(f"x_loaded{n}") for n in range(1, B)]

        def need(eng, s, v):
            if v > 0:
                eng.wait_ge(s, v)

        def normed_together(n, h):
            if n == 0:
                return slice(h * GT, (h + 1) * GT)
            return slice(0, NT) if h else None

        def span_no(n, h):
            return n + 2 if n else h + 1

        def on_vector(G, i):
            return G == NG * B - 1 and i >= GT // 2

        def shared_final(G, i):
            return G < NG * B - 1 and i % 2 == 1

        def run(parts):
            for name, *args in in_order(tuple(parts)):
                parts[name](*args)

        small_loads = [
            (kmix[:, :, k], mix_k[:, k * P:(k + 1) * P].rearrange("j p -> p j")) for k in range(KD)
        ] + [
            (knobs[:, 0:1], log_tau.partition_broadcast(P)),
            (knobs[:, 1:2], log_blend.partition_broadcast(P)),
            (knobs[:, 2:3], logit_seq.partition_broadcast(P)),
            (ema_row[:, :], ema.partition_broadcast(P)),
            (ema_col[:, :], ema.rearrange("(k p) -> p k", p=P)),
        ]
        w1_loads = []
        for k in range(KD):
            w1_loads += [
                (w1s[:, k, 0:EM].rearrange("p (e m) -> p e m", e=E),
                 W1[:, k * P:(k + 1) * P, :].rearrange("e p m -> p e m")),
                (w1s[:, k, EM:EM + M], Wo1[k * P:(k + 1) * P, :]),
            ]
        w2_loads = [
            (b1s[:, 0:NJ], b1[0:2 * NJ, :].rearrange("(j a) m -> (a m) j", a=2)),
            (b1s[0:M, NJ:NJ + 1], b1[E - 1:E, :].rearrange("o m -> m o")),
            (w2s[:, 0:NJ, :], W2[0:2 * NJ].rearrange("(j a) m d -> (a m) j d", a=2)),
            (w2s[0:M, NJ, :], W2[E - 1]),
            (w2s[M:2 * M, NJ, :], W2[E - 1]),
            (b2s[M:M + E, :], b2),
            (b2s[M + PAD:M + PAD + E, :], b2),
            (bo1s[M:2 * M, :], bo1.rearrange("(m o) -> m o", o=1)),
            (wo2s[M:2 * M, :], Wo2),
            (bo2r[:, :], bo2.partition_broadcast(P)),
            (gam[:, :], gamma.partition_broadcast(P)),
            (bet[:, :], beta.partition_broadcast(P)),
        ]

        block = ctx.enter_context(nc.Block())

        @block.sync
        def _(sp):
            xv = x.rearrange("b (t p) d -> b p t d", p=P)
            for i in range(NT // 2):
                sp.dma_start(x_sb[:, 0, 2 * i:2 * i + 2], xv[0, :, 2 * i:2 * i + 2]).then_inc(x0_loaded[i], 16)
            for dst, src in small_loads:
                sp.dma_start(dst, src, allow_slow_non_contiguous=True).then_inc(small_loaded, 16)
            for dst, src in w1_loads:
                sp.dma_start(dst, src).then_inc(w1_loaded, 16)
            sp.wait_ge(padded, 1)
            for dst, src in w2_loads:
                sp.dma_start(dst, src, allow_slow_non_contiguous=True).then_inc(w2_loaded, 16)
            for n in range(1, B):
                sp.dma_start(x_sb[:, n], xv[n]).then_inc(x_loaded[n - 1], 16)

            ov = out.rearrange("b (t p) d -> b p t d", p=P)

            def final(G, i):
                b, g = divmod(G, NG)
                t = g * GT + i
                if G == NG * B - 1:
                    sp.wait_ge(result_ready, GT // 2 * G + i + 1)
                    sp.dma_start(ov[b, :, t:t + 1], out_sb[:, b, t:t + 1]).then_inc(stored, 16)
                elif i % 2:
                    sp.wait_ge(result_ready, GT // 2 * G + i // 2 + 1)
                    sp.wait_ge(pool_result, GT // 2 * G + i // 2 + 1)
                    sp.dma_start(ov[b, :, t - 1:t + 1], out_sb[:, b, t - 1:t + 1]).then_inc(stored, 16)

            def share(G):
                g = G % NG
                sp.wait_ge(ohT_ready, G + 1)
                if G >= NG:
                    sp.wait_ge(masks_in[g], 48 * (G // NG))
                    sp.wait_ge(onehots_in[g], 32 * (G // NG))
                sp.dma_start(onehots[g], ohT[:, g]).then_inc(shared, 16)

            def fetch(G):
                g = G % NG
                sp.wait_ge(shared, 16 * (G + 1))
                need(sp, hm_done, NH * (G - 1))
                rows = onehots[g, 0:2 * NJ].rearrange("(j a) t -> a j t", a=2)
                for a in range(2):
                    sp.dma_start(mask_sb[a * M:(a + 1) * M, g],
                                 rows[a].partition_broadcast(M)).then_inc(masks_in[g], 16)
                sp.dma_start(mask8[:, g], onehots[g, E - 1].partition_broadcast(M)).then_inc(masks_in[g], 16)

            def fetch_tail(G):
                g = G % NG
                sp.wait_ge(shared, 16 * (G + 1))
                need(sp, y_ready, GT * (G - 1))
                for r in range(2):
                    sp.dma_start(tB[M + r * PAD:M + (r + 1) * PAD, g], onehots[g]).then_inc(onehots_in[g], 16)

            run({"share": share, "fetch": fetch, "fetch_tail": fetch_tail, "final": final})
            sp.wait_ge(stored, 16 * (NG * B * GT + GT) // 2)

        @block.gpsimd
        def _(pool):
            nc.gpsimd.memset(b1s[:, :], 0.0)
            nc.gpsimd.memset(b2s[:, :], 0.0).then_inc(padded, 1)
            nc.gpsimd.memset(mhalf[:, :], -0.5)
            nc.gpsimd.memset(e_base[:, :], NATURAL)
            nc.gpsimd.memset(ident[:, :], 0.0)
            nc.gpsimd.memset(ident16[:, :], 0.0)
            nc.gpsimd.memset(future16[:, :], 0.0)
            nc.gpsimd.memset(first_row[:, :], 0.0)
            nc.gpsimd.memset(not_first[:, :], 1.0).then_inc(blank, 1)
            pool.wait_ge(blank, 1)
            for m in (ident, ident16):
                nc.gpsimd.affine_select(out=m[:, :], in_=m[:, :], compare_op=ALU.not_equal, fill=1.0,
                                        base=0, pattern=[[-1, P]], channel_multiplier=1)
            nc.gpsimd.affine_select(out=future16[:, :], in_=future16[:, :], compare_op=ALU.is_gt, fill=-4.0,
                                    base=0, pattern=[[-1, P]], channel_multiplier=1)
            nc.gpsimd.affine_select(out=first_row[:, :], in_=first_row[:, :], compare_op=ALU.not_equal, fill=1.0,
                                    base=0, pattern=[[0, 1]], channel_multiplier=1)
            nc.gpsimd.affine_select(out=not_first[:, :], in_=not_first[:, :], compare_op=ALU.not_equal, fill=0.0,
                                    base=0, pattern=[[0, 1]], channel_multiplier=1)
            nc.gpsimd.iota(prio[:, :, :], pattern=[[0, GT], [-1, E]], base=E, channel_multiplier=0,
                           allow_small_or_imprecise_dtypes=True)
            nc.gpsimd.memset(xnT[:, :, 0:1], 0.0)
            nc.gpsimd.memset(xnT[:, :, T + 1:T + 2], 0.0)
            nc.gpsimd.memset(ohp[:, :, :], 0.0)
            nc.gpsimd.memset(smax[:, :, :], -8.0).then_inc(consts, 1)

            def invert(n, h):
                t = normed_together(n, h)
                if t:
                    pool.wait_ge(var_ready, span_no(n, h))
                    nc.gpsimd.tensor_tensor(rstd[:, n, t], var_e[:, t], mhalf[:, t], ALU.pow).then_inc(rstd_ready, 1)

            def ema_norm():
                pool.wait_ge(knobs_in, 1)
                nc.gpsimd.tensor_tensor(knobs_e[:, :], e_base[:, 0:3], knobs[:, :], ALU.pow).then_inc(knobs_exp, 1)
                pool.wait_ge(ema_ss, 1)
                nc.gpsimd.tensor_tensor(ema_n[:, 1:2], ema_n[:, 0:1], mhalf[:, 0:1], ALU.pow).then_inc(ema_rn, 1)

            def tap_max():
                pool.wait_ge(tap_amax, 1)
                nc.gpsimd.partition_all_reduce(gmax[:, 0:1], amax[:, 0:1], P, RMAX).then_inc(tap_gmax, 1)

            def w_max():
                pool.wait_ge(amax_ready, 1)
                nc.gpsimd.partition_all_reduce(gmax[:, 1:6], amax[:, 1:6], P, RMAX).then_inc(gmax_ready, 1)

            def w2_low():
                sub = nc.gpsimd.tensor_tensor
                pool.wait_ge(w2_split, 1)
                sub(w2l[:, :, :], w2s[:, 0:NJ, :], w2h[:, 0:NJ, :], ALU.subtract).then_inc(w2_parts, 1)
                pool.wait_ge(w2_parts, 1)
                sub(tailB[0:M, :], w2s[0:M, NJ, :], w2h[0:M, NJ, :], ALU.subtract).then_inc(w2_parts, 1)
                pool.wait_ge(w2_parts, 2)
                nc.gpsimd.tensor_copy(tailB[M:M + PAD, :], b2h[M:M + PAD, :]).then_inc(w2_parts, 1)
                pool.wait_ge(w2_parts, 3)
                sub(tailB[M + PAD:P, :], b2s[M + PAD:P, :], b2h[M + PAD:P, :], ALU.subtract).then_inc(w2_ready, 1)
                pool.wait_ge(w2_ready, 1)

            def invert_ss(n, h):
                t = normed_together(n, h)
                if t:
                    pool.wait_ge(ss_bounded, span_no(n, h))
                    nc.gpsimd.tensor_tensor(rnorm[:, n % 2, t], ss_b[:, t], mhalf[:, t], ALU.pow).then_inc(rn_ready, 1)

            def mix_lo(n, c):
                h, k = divmod(c, KD)
                cols = slice(h * GW, (h + 1) * GW)
                pool.wait_ge(xh_done, CHUNKS * n + c + 1)
                nc.gpsimd.tensor_tensor(xmT[:, n % 2, KD + k, cols], mixt[:, c], xmT[:, n % 2, k, cols],
                                        ALU.subtract).then_inc(xl_done, 1)

            def exponent(b):
                pool.wait_ge(expo_ready, b + 1)
                need(pool, gate_ready, b)
                nc.gpsimd.tensor_tensor(novelty[:, :], e_base[:, :], expo[:, :], ALU.pow).then_inc(nov_ready, 1)

            def low(G, q):
                g, m = G % NG, NH * G + q
                pool.wait_ge(hi_done, m + 1)
                nc.gpsimd.tensor_tensor(hl[:, g, q - 1], hm[:, m % 4], hh[:, g, q - 1],
                                        ALU.subtract).then_inc(lo_done, 1)

            def z_invert(G):
                g = G % NG
                pool.wait_ge(zve_ready, G + 1)
                nc.gpsimd.tensor_tensor(zr[:, g], zve[:, g], mhalf[:, 0:GT], ALU.pow).then_inc(zr_ready, 1)

            def times_gamma(G, i):
                g, Y = G % NG, GT * G + i
                if on_vector(G, i):
                    return
                pool.wait_ge(w_norm, Y + 1)
                nc.gpsimd.tensor_tensor(z[:, g, i], z[:, g, i], gam[:, :], ALU.mult).then_inc(w_gamma, 1)

            def plus_beta(G, i):
                g, Y = G % NG, GT * G + i
                if on_vector(G, i):
                    return
                pool.wait_ge(w_gamma, Y + 1)
                nc.gpsimd.tensor_tensor(z[:, g, i], z[:, g, i], bet[:, :], ALU.add).then_inc(w_affine, 1)

            def final(G, i):
                b, g = divmod(G, NG)
                t, Y = g * GT + i, GT * G + i
                if shared_final(G, i):
                    pool.wait_ge(gated, Y + 1)
                    pool.wait_ge(w_affine, Y + 1)
                    nc.gpsimd.tensor_tensor(out_sb[:, b, t], out_sb[:, b, t], z[:, g, i],
                                            ALU.add).then_inc(pool_result, 1)

            run({"final": final, "invert": invert, "ema_norm": ema_norm, "tap_max": tap_max, "w_max": w_max,
                 "w2_low": w2_low, "invert_ss": invert_ss, "mix_lo": mix_lo, "exponent": exponent, "low": low,
                 "z_invert": z_invert, "times_gamma": times_gamma, "plus_beta": plus_beta})

        @block.scalar
        def _(act):
            def w1_high():
                act.wait_ge(scales_ready, 1)
                nc.scalar.activation(w1h[:, :, EM:EM + M], w1s[:, :, EM:EM + M], ACT.Copy, scale=sc[:, 7:8])
                nc.scalar.activation(w1h[:, :, 0:EM], w1s[:, :, 0:EM], ACT.Copy, scale=sc[:, 3:4]).then_inc(w1_split, 1)

            def w2_high():
                act.wait_ge(scales_ready, 1)
                nc.scalar.activation(w2h[:, :, :], w2s[:, :, :], ACT.Copy, scale=sc[:, 10:11])
                nc.scalar.activation(b2h[:, :], b2s[:, :], ACT.Copy, scale=sc[:, 12:13])
                nc.scalar.activation(w2s[:, :, :], w2s[:, :, :], ACT.Copy, scale=sc[:, 10:11])
                nc.scalar.activation(b2s[:, :], b2s[:, :], ACT.Copy, scale=sc[:, 12:13]).then_inc(w2_split, 1)

            def gelu(n, t):
                X = NT * n + t
                act.wait_ge(xn_ready, X + 1)
                nc.scalar.activation(out_sb[:, n, t], xn_st[:, t % 4], ACT.Gelu_apprx_tanh).then_inc(gelu_done, 1)

            def square(n, t):
                S = NT * n + t
                act.wait_ge(gelu_done, S + 1)
                need(act, ss_ready, S - 1)
                if n and t == 0:
                    act.wait_ge(ss_bounded, span_no(n - 1, 1))
                nc.scalar.activation(junk[:, t % 2], out_sb[:, n, t], ACT.Square,
                                     accum_out=ss[:, t:t + 1]).then_inc(ss_ready, 1)

            def keep_x(n, t):
                act.wait_ge(tx_done, NT * n + t + 1)
                if n and (t == 0 or t == GT - 1):
                    act.wait_ge(m2_done, CHUNKS * (n - 1) + KD * ((t + 1) // GT + 1))
                nc.scalar.copy(xnT[:, :, 1 + t * P:1 + (t + 1) * P],
                               rows_in(short("transpose", n, t))).then_inc(xe_done, 1)

            def unit(n, t):
                X = NT * n + t
                if t % GT == 0:
                    act.wait_ge(rn_ready, span_no(n, t // GT))
                need(act, tu_done, X - 3)
                nc.scalar.activation(unit_st[:, t % 4], out_sb[:, n, t], ACT.Copy,
                                     scale=rnorm[:, n % 2, t:t + 1]).then_inc(unit_ready, 1)

            def unit_hi(n, t):
                act.wait_ge(tu_done, NT * n + t + 1)
                if t == 0:
                    need(act, sim_ready, NP * (n - 1))
                    need(act, ema_ready, n - 1)
                nc.scalar.copy(uT[:, n % 2, 0:KD, t * P:(t + 1) * P],
                               rows_in(short("unit_turn", n, t))).then_inc(uh_ready, 1)

            def tap0(n, c):
                h, k = divmod(c, KD)
                if k == 0:
                    act.wait_ge(xe_done, NT * n + min(NT, GT * (h + 1) + 1))
                if c == 0:
                    act.wait_ge(taps_ready, 1)
                need(act, xl_done, CHUNKS * (n - 1) + c + 1)
                nc.scalar.activation(mixt[:, c], xnT[:, k, h * GW:(h + 1) * GW], ACT.Copy,
                                     scale=kmix_s[:, 0, k:k + 1]).then_inc(m0_done, 1)

            def mix_hi(n, c):
                h, k = divmod(c, KD)
                act.wait_ge(m2_done, CHUNKS * n + c + 1)
                if c == 0 and n >= 2:
                    act.wait_ge(h_ready, HIDDEN.index(("hidden", NG * (n - 1) - 1, NJ)) + 1)
                nc.scalar.copy(xmT[:, n % 2, k, h * GW:(h + 1) * GW], mixt[:, c]).then_inc(xh_done, 1)

            def tanh(G):
                H = HIDDEN.index(("router", G))
                act.wait_ge(h_ready, H + 1)
                need(act, sco_ready, G)
                nc.scalar.activation(sT[M:2 * M, :], hP[H % 2][M:2 * M, :], ACT.Tanh,
                                     bias=bo1s[M:2 * M, :], scale=sc[M:2 * M, 8:9]).then_inc(tanh_done, 1)

            def keep_h8(G):
                H = HIDDEN.index(("router", G))
                act.wait_ge(h_ready, H + 1)
                need(act, hm_done, NH * (G - 1) + 1)
                nc.scalar.copy(h8[:, :], hP[H % 2][0:M, :]).then_inc(h8_done, 1)

            def keep_pick(G):
                act.wait_ge(ohTP_ready, G + 1)
                need(act, shared, 16 * (G - 1))
                nc.scalar.copy(ohT[:, G % 2], short("pick", G)[0:PAD, :]).then_inc(ohT_ready, 1)

            def high(G, q):
                g = G % NG
                m = NH * G + q
                act.wait_ge(hm_done, m + 1)
                if q == 0:
                    need(act, y_ready, GT * (G - 1))
                    nc.scalar.copy(tB[0:M, g], hm[0:M, m % 4])
                    nc.scalar.copy(tA[0:M, g], hm[0:M, m % 4]).then_inc(hi_done, 1)
                else:
                    nc.scalar.copy(hh[:, g, q - 1], hm[:, m % 4]).then_inc(hi_done, 1)

            def affine(G, i):
                g = G % NG
                act.wait_ge(zb_ready, G + 1)
                nc.scalar.activation(z[:, g, i], z[:, g, i], ACT.Identity, bias=zb[:, g, i:i + 1],
                                     scale=zr[:, g, i:i + 1]).then_inc(w_norm, 1)

            run({"w1_high": w1_high, "w2_high": w2_high, "gelu": gelu, "square": square, "keep_x": keep_x,
                 "tap0": tap0, "mix_hi": mix_hi, "unit": unit, "unit_hi": unit_hi, "tanh": tanh,
                 "keep_h8": keep_h8, "keep_pick": keep_pick, "high": high, "affine": affine})

        @block.vector
        def _(dve):
            ts = nc.vector.tensor_scalar
            stt = nc.vector.scalar_tensor_tensor
            tt = nc.vector.tensor_tensor
            count = [0]

            def mark(ins):
                count[0] += 1
                ins.then_inc(own_setup, 1)

            def link(ins):
                mark(ins)
                dve.wait_ge(own_setup, count[0])

            def col(i):
                return sc[:, i:i + 1]

            def ema_norm():
                dve.wait_ge(small_loaded, 16 * len(small_loads))
                ts(knobs[:, 1:3], knobs[:, 1:3], -1.0, None, ALU.mult).then_inc(knobs_in, 1)
                link(tt(ema_sq[:, :], ema_row[:, :], ema_row[:, :], ALU.mult))
                link(nc.vector.reduce_sum(ema_n[:, 0:1], ema_sq[:, :], AX.X))
                ts(ema_n[:, 0:1], ema_n[:, 0:1], NORM_MIN * NORM_MIN, None, ALU.max).then_inc(ema_ss, 1)

            def tap_max():
                dve.wait_ge(small_loaded, 16 * len(small_loads))
                link(nc.vector.tensor_reduce(kabs[:, :], kmix[:, :, :].rearrange("p j k -> p k j"), AX.X, ALU.add,
                                             apply_absolute_value=True))
                nc.vector.reduce_max(amax[:, 0:1], kabs[:, :], AX.X).then_inc(tap_amax, 1)

            def tap_scale():
                dve.wait_ge(tap_gmax, 1)
                link(ts(col(0), gmax[:, 0:1], SCALE_MIN, None, ALU.max))
                link(nc.vector.reciprocal(col(1), col(0)))
                ts(kmix_s[:, :, :], kmix[:, :, :], col(1), None, ALU.mult).then_inc(taps_ready, 1)

            def constants():
                dve.wait_ge(knobs_exp, 1)
                link(ts(tau[:, 3:5], knobs_e[:, 1:3], 1.0, None, ALU.add))
                link(nc.vector.reciprocal(tau[:, 5:7], tau[:, 3:5]))
                nc.vector.tensor_copy(tau[:, 1:2], tau[:, 5:6])
                ts(tau[:, 2:3], tau[:, 5:6], -1.0, 1.0, ALU.mult, ALU.add)
                link(ts(tau[:, 7:8], knobs_e[:, 0:1], -1.0, None, ALU.mult))
                link(tt(tau[:, 3:4], tau[:, 6:7], tau[:, 7:8], ALU.mult))
                link(tt(tau[:, 4:5], tau[:, 7:8], tau[:, 3:4], ALU.subtract))
                dve.wait_ge(ema_rn, 1)
                link(ts(ema_col[:, :], ema_col[:, :], ema_n[:, 1:2], None, ALU.mult))
                link(nc.vector.tensor_copy(ema_hl[:, :, 0], ema_col[:, :]))
                tt(ema_hl[:, :, 1], ema_col[:, :], ema_hl[:, :, 0], ALU.subtract).then_inc(ema_split, 1)

            def w_max():
                dve.wait_ge(w1_loaded, 16 * len(w1_loads))
                nc.vector.tensor_reduce(amax[:, 1:2], w1s[:, :, 0:EM], AX.XY, ALU.max, apply_absolute_value=True)
                nc.vector.tensor_reduce(amax[:, 2:3], w1s[:, :, EM:EM + M], AX.XY, ALU.max, apply_absolute_value=True)
                dve.wait_ge(w2_loaded, 16 * len(w2_loads))
                nc.vector.tensor_reduce(amax[:, 3:4], w2s[:, :, :], AX.XY, ALU.max, apply_absolute_value=True)
                nc.vector.tensor_reduce(amax[:, 4:5], b1s[:, :], AX.X, ALU.max, apply_absolute_value=True)
                nc.vector.tensor_reduce(amax[:, 5:6], b2s[:, :], AX.X, ALU.max,
                                        apply_absolute_value=True).then_inc(amax_ready, 1)

            def w_scale():
                dve.wait_ge(gmax_ready, 1)
                dve.wait_ge(taps_ready, 1)
                ts(col(6), gmax[:, 2:3], SCALE_MIN, None, ALU.max)
                link(ts(col(2), gmax[:, 4:5], col(1), SCALE_MIN, ALU.mult, ALU.max))
                link(tt(col(2), col(2), gmax[:, 1:2], ALU.max))
                nc.vector.reciprocal(col(7), col(6))
                tt(col(8), col(6), col(0), ALU.mult)
                nc.vector.reciprocal(col(3), col(2))
                link(tt(col(4), col(2), col(0), ALU.mult))
                link(nc.vector.reciprocal(col(5), col(4)))
                link(ts(col(9), gmax[:, 5:6], col(5), SCALE_MIN, ALU.mult, ALU.max))
                link(tt(col(9), col(9), gmax[:, 3:4], ALU.max))
                nc.vector.reciprocal(col(10), col(9))
                link(tt(col(11), col(4), col(9), ALU.mult))
                link(nc.vector.reciprocal(col(12), col(11)))
                link(tt(col(13), col(12), col(12), ALU.mult))
                ts(b1n[:, :], b1s[:, :], col(5), None, ALU.mult)
                ts(col(13), col(13), LN_EPS, None, ALU.mult).then_inc(scales_ready, 1)

            def w1_low():
                dve.wait_ge(w1_split, 1)
                stt(w1l[:, :, 0:EM], w1s[:, :, 0:EM], col(3), w1h[:, :, 0:EM], ALU.mult, ALU.subtract)
                stt(w1l[:, :, EM:EM + M], w1s[:, :, EM:EM + M], col(7), w1h[:, :, EM:EM + M], ALU.mult,
                    ALU.subtract).then_inc(w1_ready, 1)

            def row_stats(n, t):
                if n:
                    if t == 0:
                        dve.wait_ge(x_loaded[n - 1], 16)
                elif t % 2 == 0:
                    dve.wait_ge(x0_loaded[t // 2], 16)
                nc.vector.bn_stats(stats[:, n % 2, t], x_sb[:, n, t]).then_inc(st_ready, 1)

            def variance(n, h):
                rows = normed_together(n, h)
                if not rows:
                    return
                dve.wait_ge(st_ready, NT * n + rows.stop)
                for t in range(rows.start, rows.stop):
                    last = nc.vector.bn_aggr(mv[:, n % 2, t], stats[:, n % 2, t])
                last.then_inc(mv_ready, 1)
                dve.wait_ge(mv_ready, span_no(n, h))
                if n:
                    dve.wait_ge(rstd_ready, span_no(n - 1, 1))
                ts(var_e[:, rows], mv[:, n % 2, rows, 1], LN_EPS, None, ALU.add).then_inc(var_ready, 1)

            def shift(n, h):
                rows = normed_together(n, h)
                if rows:
                    dve.wait_ge(rstd_ready, span_no(n, h))
                    stt(nbias[:, n % 2, rows], mv[:, n % 2, rows, 0], -1.0, rstd[:, n, rows], ALU.mult,
                        ALU.mult).then_inc(nb_ready, 1)

            def norm(n, t):
                X = NT * n + t
                dve.wait_ge(nb_ready, span_no(n, t // GT))
                need(dve, tx_done, X - 3)
                need(dve, gelu_done, X - 3)
                ts(xn_st[:, t % 4], x_sb[:, n, t], rstd[:, n, t:t + 1], nbias[:, n % 2, t:t + 1],
                   ALU.mult, ALU.add).then_inc(xn_ready, 1)

            def bound_ss(n, h):
                rows = normed_together(n, h)
                if rows:
                    dve.wait_ge(ss_ready, NT * n + rows.stop)
                    ts(ss_b[:, rows], ss[:, rows], NORM_MIN * NORM_MIN, None, ALU.max).then_inc(ss_bounded, 1)

            def unit_lo(n, t):
                dve.wait_ge(uh_ready, NT * n + t + 1)
                u = uT[:, n % 2, :, t * P:(t + 1) * P]
                tt(u[:, KD:2 * KD], rows_in(short("unit_turn", n, t)), u[:, 0:KD], ALU.subtract).then_inc(ue_done, 1)

            def tap1(n, c):
                h, k = divmod(c, KD)
                dve.wait_ge(m0_done, CHUNKS * n + c + 1)
                stt(mixt[:, c], xnT[:, k, 1 + h * GW:1 + (h + 1) * GW], kmix_s[:, 1, k:k + 1], mixt[:, c],
                    ALU.mult, ALU.add).then_inc(m1_done, 1)

            def tap2(n, c):
                h, k = divmod(c, KD)
                dve.wait_ge(m1_done, CHUNKS * n + c + 1)
                stt(mixt[:, c], xnT[:, k, 2 + h * GW:2 + (h + 1) * GW], kmix_s[:, 2, k:k + 1], mixt[:, c],
                    ALU.mult, ALU.add).then_inc(m2_done, 1)

            def inv_(b):
                dve.wait_ge(scales_ready, 1)
                ts(inv[:, b], rstd[:, b], sc[:, 12:13], None, ALU.mult).then_inc(inv_ready, 1)

            def ema_sum(b):
                dve.wait_ge(ema_ready, b + 1)
                need(dve, expo_ready, b)
                nc.vector.reduce_sum(ems[:, :], ema_in(short("ema_dot", b)), AX.X).then_inc(ems_ready, 1)

            def sim_max(b, q):
                t, lo, hi = PIECES[q]
                if q == 0:
                    need(dve, expo_ready, b)
                dve.wait_ge(sim_ready, NP * b + q + 1)
                nc.vector.reduce_max(smax[:, t, lo // 4:lo // 4 + 1], simP[q % 2][:, 0:(hi - lo) * P],
                                     AX.X).then_inc(sim_free, 1)

            def familiar(b):
                n = [0]

                def chain(ins):
                    n[0] += 1
                    ins.then_inc(own_gate, 1)
                    dve.wait_ge(own_gate, 4 * b + n[0])

                dve.wait_ge(ema_split, 1)
                dve.wait_ge(sim_free, NP * b + NP)
                dve.wait_ge(ems_ready, b + 1)
                need(dve, nov_ready, b)
                chain(tt(seq[:, :], smax[:, :, 0], smax[:, :, 1], ALU.max))
                chain(ts(fix[:, :], ems[:, 0:1], first_row[:, :], None, ALU.mult))
                chain(stt(seq[:, 0:1], seq[:, 0:1], not_first[:, :], fix[:, :], ALU.mult, ALU.add))
                chain(ts(seq[:, :], seq[:, :], tau[:, 3:4], None, ALU.mult))
                stt(expo[:, :], ems[:, :], tau[:, 4:5], seq[:, :], ALU.mult, ALU.add).then_inc(expo_ready, 1)

            def gate_(b):
                dve.wait_ge(nov_ready, b + 1)
                ts(gate[:, b], novelty[:, :], tau[:, 1:2], tau[:, 2:3], ALU.mult, ALU.add).then_inc(gate_ready, 1)

            def argmax(G, i):
                def over(v):
                    return v.to_broadcast([P, GT, E])

                if i == 0:
                    dve.wait_ge(sco_ready, G + 1)
                    need(dve, ohTP_ready, G)
                else:
                    dve.wait_ge(own_argmax, 5 * G + i)
                if i == 0:
                    step = tt(sco[:, :, :], scores_in(short("scores", G)),
                              bo2r[:, :].unsqueeze(1).to_broadcast([P, GT, E]), ALU.add)
                elif i == 1:
                    step = nc.vector.reduce_max(top[:, :, 0], sco[:, :, :], AX.X)
                elif i == 2:
                    step = tt(sco[:, :, :], sco[:, :, :], over(top[:, :, 0:1]), ALU.is_ge)
                elif i == 3:
                    step = tt(sco[:, :, :], sco[:, :, :], prio[:, :, :], ALU.mult)
                elif i == 4:
                    step = nc.vector.reduce_max(top[:, :, 1], sco[:, :, :], AX.X)
                else:
                    step = tt(ohp[:, :, 0:E], sco[:, :, :], over(top[:, :, 1:2]), ALU.is_equal)
                step.then_inc(own_argmax if i < 5 else oh_ready, 1)

            def masked(G, q):
                m, g = NH * G + q, G % NG
                if q == 0:
                    dve.wait_ge(masks_in[g], 48 * (G // NG + 1))
                if m >= 4:
                    G2, q2 = divmod(m - 4, NH)
                    if q2:
                        dve.wait_ge(lo_done, NJ * G2 + q2)
                    else:
                        dve.wait_ge(lo8_done, G2 + 1)
                if q == 0:
                    dve.wait_ge(h8_done, G + 1)
                    stt(hm[0:M, m % 4], h8[:, :], b1n[0:M, NJ:NJ + 1], mask8[:, g],
                        ALU.add, ALU.mult).then_inc(hm_done, 1)
                else:
                    H = HIDDEN.index(("hidden", G, q))
                    dve.wait_ge(h_ready, H + 1)
                    stt(hm[:, m % 4], hP[H % 2][:, :], b1n[:, q - 1:q], mask_sb[:, g, q - 1],
                        ALU.add, ALU.mult).then_inc(hm_done, 1)

            def low8(G):
                m = NH * G
                dve.wait_ge(hi_done, m + 1)
                tt(tA[M:2 * M, G % NG], hm[0:M, m % 4], tA[0:M, G % NG], ALU.subtract).then_inc(lo8_done, 1)

            def residual(G, i):
                b, g = divmod(G, NG)
                Y = GT * G + i
                dve.wait_ge(y_ready, Y + 1)
                if G >= NG:
                    dve.wait_ge(pool_result if i % 2 else result_ready, (G - NG) * GT // 2 + i // 2 + 1)
                if i == 0:
                    dve.wait_ge(inv_ready, b + 1)
                stt(z[:, g, i], x_sb[:, b, g * GT + i], inv[:, b, g * GT + i:g * GT + i + 1], yP[:, :], ALU.mult,
                    ALU.add).then_inc(z_done, 1)

            def z_stats(G, i):
                dve.wait_ge(z_done, GT * G + i + 1)
                need(dve, zmv_ready, G - 1)
                nc.vector.bn_stats(zst[:, G % NG, i], z[:, G % NG, i]).then_inc(zst_ready, 1)

            def z_var(G):
                g = G % NG
                dve.wait_ge(zst_ready, GT * G + GT)
                for i in range(GT):
                    last = nc.vector.bn_aggr(zmv[:, g, i], zst[:, g, i])
                last.then_inc(zmv_ready, 1)
                dve.wait_ge(zmv_ready, G + 1)
                ts(zve[:, g], zmv[:, g, :, 1], sc[:, 13:14], None, ALU.add).then_inc(zve_ready, 1)

            def z_shift(G):
                g = G % NG
                dve.wait_ge(zr_ready, G + 1)
                stt(zb[:, g], zmv[:, g, :, 0], -1.0, zr[:, g], ALU.mult, ALU.mult).then_inc(zb_ready, 1)

            def times_gamma(G, i):
                if on_vector(G, i):
                    dve.wait_ge(w_norm, GT * G + i + 1)
                    tt(z[:, G % NG, i], z[:, G % NG, i], gam[:, :], ALU.mult).then_inc(last_gamma, 1)

            def plus_beta(G, i):
                if on_vector(G, i):
                    dve.wait_ge(last_gamma, i + 1 - GT // 2)
                    tt(z[:, G % NG, i], z[:, G % NG, i], bet[:, :], ALU.add).then_inc(last_affine, 1)

            def gated_(G, i):
                b, g = divmod(G, NG)
                t = g * GT + i
                dve.wait_ge(gate_ready, b + 1)
                stt(out_sb[:, b, t], out_sb[:, b, t], gate[:, b, t:t + 1], x_sb[:, b, t],
                    ALU.mult, ALU.add).then_inc(gated, 1)

            def final(G, i):
                b, g = divmod(G, NG)
                t = g * GT + i
                Y = GT * G + i
                if shared_final(G, i):
                    return
                if on_vector(G, i):
                    dve.wait_ge(last_affine, i + 1 - GT // 2)
                else:
                    dve.wait_ge(w_affine, Y + 1)
                dve.wait_ge(gated, Y + 1)
                tt(out_sb[:, b, t], out_sb[:, b, t], z[:, g, i], ALU.add).then_inc(result_ready, 1)

            run({"ema_norm": ema_norm, "tap_max": tap_max, "tap_scale": tap_scale, "constants": constants,
                 "w_max": w_max, "w_scale": w_scale, "w1_low": w1_low, "row_stats": row_stats,
                 "variance": variance, "shift": shift, "norm": norm, "bound_ss": bound_ss, "unit_lo": unit_lo,
                 "tap1": tap1, "tap2": tap2, "inv": inv_, "ema_sum": ema_sum, "sim_max": sim_max,
                 "familiar": familiar, "gate": gate_, "argmax": argmax, "masked": masked, "low8": low8,
                 "residual": residual, "z_stats": z_stats, "z_var": z_var, "z_shift": z_shift,
                 "times_gamma": times_gamma, "plus_beta": plus_beta, "gated": gated_, "final": final})

        @block.tensor
        def _(pe):
            mm = nc.tensor.matmul

            def short_free(*use):
                S = SHORT.index(use)
                if S < 3:
                    return
                name, *args = SHORT[S - 3]
                n = args[0]
                if name == "transpose":
                    pe.wait_ge(xe_done, NT * n + args[1] + 1)
                elif name == "unit_turn":
                    pe.wait_ge(ue_done, NT * n + args[1] + 1)
                elif name == "scores":
                    pe.wait_ge(own_argmax, 5 * n + 1)
                elif name == "ema_dot":
                    pe.wait_ge(ems_ready, n + 1)
                else:
                    pe.wait_ge(ohT_ready, n + 1)

            def transpose(n, t):
                X = NT * n + t
                if X == 0:
                    pe.wait_ge(consts, 1)
                pe.wait_ge(xn_ready, X + 1)
                short_free("transpose", n, t)
                rows = rows_in(short("transpose", n, t))
                for k in range(KD):
                    last = nc.tensor.transpose(rows[:, k], xn_st[:, t % 4, k * P:(k + 1) * P], ident[:, :])
                last.then_inc(tx_done, 1)

            def unit_turn(n, t):
                pe.wait_ge(unit_ready, NT * n + t + 1)
                short_free("unit_turn", n, t)
                rows = rows_in(short("unit_turn", n, t))
                for k in range(KD):
                    last = nc.tensor.transpose(rows[:, k], unit_st[:, t % 4, k * P:(k + 1) * P], ident[:, :])
                last.then_inc(tu_done, 1)

            def ema_dot(b):
                u = uT[:, b % 2]
                pe.wait_ge(ue_done, NT * b + NT)
                pe.wait_ge(ema_split, 1)
                short_free("ema_dot", b)
                sums = ema_in(short("ema_dot", b))
                for t in range(NT):
                    for n, (i, k) in enumerate((i, k) for i in range(2) for k in range(KD)):
                        last = mm(sums[:, t], u[:, i * KD + k, t * P:(t + 1) * P], ema_hl[:, k, :],
                                  start=(n == 0), stop=(n == 2 * KD - 1))
                last.then_inc(ema_ready, 1)

            def sim(b, q):
                t, lo, hi = PIECES[q]
                u = uT[:, b % 2]
                pe.wait_ge(ue_done, NT * b + t + 1)
                need(pe, sim_free, NP * b + q - 1)
                w = (hi - lo) * P
                bank = simP[q % 2]
                terms = [(i, j, k) for i, j in PAIRS for k in range(KD)]
                for n, (i, j, k) in enumerate(terms):
                    last = mm(bank[:, 0:w], u[:, i * KD + k, t * P:(t + 1) * P],
                              u[:, j * KD + k, lo * P:hi * P], start=(n == 0), stop=(n == len(terms) - 1))
                    if n == 0 and hi == t + 1:
                        mm(bank[:, w - P:w], ident16[:, :], future16[:, :], start=False, stop=False)
                last.then_inc(sim_ready, 1)

            def hidden(G, q):
                b, g = divmod(G, NG)
                H = HIDDEN.index(("hidden", G, q) if q else ("router", G))
                if H >= 2:
                    name, *old = HIDDEN[H - 2]
                    if name == "hidden":
                        pe.wait_ge(hm_done, NH * old[0] + old[1] + 1)
                    else:
                        pe.wait_ge(h8_done, old[0] + 1)
                        pe.wait_ge(tanh_done, old[0] + 1)
                cols = slice(NJ * 2 * M, NJ * 2 * M + P) if q == 0 else slice((q - 1) * P, q * P)
                terms = [(i, j, k) for i, j in PAIRS for k in range(KD)]
                for n, (i, j, k) in enumerate(terms):
                    last = mm(hP[H % 2][:, :], (w1h, w1l)[i][:, k, cols],
                              xmT[:, b % 2, j * KD + k, g * GW:(g + 1) * GW], start=(n == 0),
                              stop=(n == len(terms) - 1))
                last.then_inc(h_ready, 1)

            def router(G):
                b, g = divmod(G, NG)
                pe.wait_ge(w1_ready, 1)
                pe.wait_ge(xl_done, CHUNKS * b + KD * (g + 1))
                hidden(G, 0)

            def scores(G):
                pe.wait_ge(tanh_done, G + 1)
                short_free("scores", G)
                bank = scores_in(short("scores", G))
                for i in range(GT):
                    last = mm(bank[:, i], sT[M:2 * M, i * P:(i + 1) * P], wo2s[M:2 * M, :], start=True, stop=True)
                last.then_inc(sco_ready, 1)

            def pick_(G):
                pe.wait_ge(oh_ready, G + 1)
                short_free("pick", G)
                bank = short("pick", G)
                for i in range(GT):
                    last = mm(bank[0:PAD, i * P:(i + 1) * P], ohp[:, i, :], ident16[:, :], start=True, stop=True)
                last.then_inc(ohTP_ready, 1)

            def expert(G, i):
                g = G % NG
                Y = GT * G + i
                need(pe, z_done, Y)
                if i == 0:
                    pe.wait_ge(lo8_done, G + 1)
                    pe.wait_ge(lo_done, NJ * (G + 1))
                    pe.wait_ge(onehots_in[g], 32 * (G // NG + 1))
                    pe.wait_ge(w2_ready, 1)
                cols = slice(i * P, (i + 1) * P)
                mm(yP[:, :], tA[:, g, cols], w2h[:, NJ], start=True, stop=False)
                mm(yP[:, :], tB[:, g, cols], tailB[:, :], start=False, stop=False)
                for j in range(NJ):
                    mm(yP[:, :], hh[:, g, j, cols], w2h[:, j], start=False, stop=False)
                    mm(yP[:, :], hl[:, g, j, cols], w2h[:, j], start=False, stop=False)
                    last = mm(yP[:, :], hh[:, g, j, cols], w2l[:, j], start=False, stop=(j == NJ - 1))
                last.then_inc(y_ready, 1)

            run({"transpose": transpose, "unit_turn": unit_turn, "ema_dot": ema_dot, "sim": sim,
                 "hidden": hidden, "router": router, "scores": scores, "pick": pick_, "expert": expert})


_INS = ["L0_attn_x", "L0_attn_ema_out", "L0_attn_log_tau", "L0_attn_log_blend", "L0_attn_logit_blend_seq",
        "L0_ffn_mix_kernel", "L0_ffn_W1", "L0_ffn_b1", "L0_ffn_W2", "L0_ffn_b2", "L0_ffn_Wo1", "L0_ffn_bo1",
        "L0_ffn_Wo2", "L0_ffn_bo2", "L0_ffn_gamma", "L0_ffn_beta"]


def kernel(**inputs):
    import numpy as _np
    import concourse.bacc as _bacc
    from concourse import mybir as _mybir
    from concourse.bass_utils import run_bass_kernel_spmd as _run

    nc = _bacc.Bacc("TRN2", target_bir_lowering=False, num_devices=1)
    arrays, args = {}, []
    for name in _INS:
        a = _np.ascontiguousarray(inputs[name])
        if a.ndim == 0:
            a = a.reshape(1)
        arrays[f"in_{name}"] = a
        args.append(nc.dram_tensor(f"in_{name}", a.shape, _mybir.dt.from_np(a.dtype), kind="ExternalInput").ap())
    shape = arrays["in_L0_attn_x"].shape
    out = nc.dram_tensor("out_0", shape, _mybir.dt.float32, kind="ExternalOutput").ap()
    build(nc, *args, out)
    r = _run(nc, [arrays], core_ids=[0])
    return r.results[0]["out_0"]
```
